# Optimizing a Trainium2 kernel written in Bass

```python
import numpy as np
import jax
import jax.numpy as jnp

def _softmax(x, axis=-1):
    return jax.nn.softmax(x, axis=axis)

def _gelu(x):
    return jax.nn.gelu(x, approximate=True)

def _silu(x):
    return jax.nn.silu(x)

def _sigmoid(x):
    return jax.nn.sigmoid(x)

def _layernorm(x, axis=-1, eps=1e-05):
    m = jnp.mean(x, axis=axis, keepdims=True)
    v = jnp.var(x, axis=axis, keepdims=True)
    return (x - m) / jnp.sqrt(v + eps)

def _scatter_add(tgt, idx, src, axis=0):
    return tgt.at[idx].add(src)

def _segment_sum(src, seg, n):
    return jax.ops.segment_sum(src, seg, n)
kernel_name = 'mk_recurrent_d1_jaxref_r8_b9789c'

def setup_inputs(seed: int=0):
    np.random.seed(seed)
    _w = jnp.asarray

    def _L0_attn_setup():
        import jax, jax.numpy as jnp
        import numpy as np
        import math
        B, T, D_IN, D_OUT = (2, 256, 512, 512)
        N_HEADS, N_KV = (32, 8)
        HEAD_DIM = D_OUT // N_HEADS
        GROUP_SIZE = N_HEADS // N_KV
        ROPE_BASE = 500000.0
        CTX = 256

        def _rope_tables(head_dim, base, seq_len):
            inv_freq = 1.0 / base ** (jnp.arange(0, head_dim, 2, dtype=jnp.float32) / head_dim)
            t = jnp.arange(seq_len, dtype=jnp.float32)
            freqs = jnp.einsum('i,j->ij', t, inv_freq)
            return (jnp.cos(freqs), jnp.sin(freqs))

        def _apply_rope(x, cos, sin):
            x1, x2 = jnp.split(x, 2, axis=-1)
            c = cos[None, None]
            s = sin[None, None]
            return jnp.concatenate([x1 * c - x2 * s, x1 * s + x2 * c], axis=-1)
        key = jax.random.key(seed)
        ks = jax.random.split(key, 5)
        scale = 0.02
        return {'x': jax.random.normal(ks[0], (B, T, D_IN), dtype=jnp.float32), 'Wq': jax.random.normal(ks[1], (D_IN, D_OUT), dtype=jnp.float32) * scale, 'Wk': jax.random.normal(ks[2], (D_IN, N_KV * HEAD_DIM), dtype=jnp.float32) * scale, 'Wv': jax.random.normal(ks[3], (D_IN, N_KV * HEAD_DIM), dtype=jnp.float32) * scale, 'Wo': jax.random.normal(ks[4], (D_OUT, D_OUT), dtype=jnp.float32) * scale}
    _L0_attn_in = _L0_attn_setup()

    def _L0_ffn_setup():
        import jax, jax.numpy as jnp
        import numpy as np
        GROUP_SIZE = 128
        THRESHOLD = 0.5
        EPS = 1e-08

        def ternary_quantize_groupwise(w):
            out_f, in_f = w.shape
            num_groups = in_f // GROUP_SIZE
            g = w.reshape(out_f, num_groups, GROUP_SIZE)
            scale = jnp.maximum(jnp.mean(jnp.abs(g), axis=-1, keepdims=True), EPS)
            w_norm = g / scale
            q = jnp.where(w_norm > THRESHOLD, 1.0, jnp.where(w_norm < -THRESHOLD, -1.0, 0.0))
            return (q * scale).reshape(out_f, in_f)
        key = jax.random.key(seed)
        k1, k2 = jax.random.split(key)
        x = jax.random.normal(k1, (2, 256, 512), dtype=jnp.float32)
        weight = jax.random.normal(k2, (512, 512), dtype=jnp.float32)
        return {'x': x, 'weight': weight}
    _L0_ffn_in = _L0_ffn_setup()
    _d = {'L0_attn_x': _L0_attn_in['x'], 'L0_attn_Wq': _L0_attn_in['Wq'], 'L0_attn_Wk': _L0_attn_in['Wk'], 'L0_attn_Wv': _L0_attn_in['Wv'], 'L0_attn_Wo': _L0_attn_in['Wo'], 'L0_ffn_weight': _L0_ffn_in['weight']}
    _x0 = _d['L0_attn_x']
    _d['L0_attn_x'] = jax.random.normal(jax.random.fold_in(jax.random.key(seed), 1), (1, 1024, 512), dtype=_x0.dtype)
    del _x0
    return _d

def reference(L0_attn_x, L0_attn_Wq, L0_attn_Wk, L0_attn_Wv, L0_attn_Wo, L0_ffn_weight):

    def _L0_attn_ref(x, Wq, Wk, Wv, Wo):
        import jax, jax.numpy as jnp
        import numpy as np
        import math
        B, T, D_IN, D_OUT = (2, 256, 512, 512)
        N_HEADS, N_KV = (32, 8)
        HEAD_DIM = D_OUT // N_HEADS
        GROUP_SIZE = N_HEADS // N_KV
        ROPE_BASE = 500000.0
        CTX = 256

        def _rope_tables(head_dim, base, seq_len):
            inv_freq = 1.0 / base ** (jnp.arange(0, head_dim, 2, dtype=jnp.float32) / head_dim)
            t = jnp.arange(seq_len, dtype=jnp.float32)
            freqs = jnp.einsum('i,j->ij', t, inv_freq)
            return (jnp.cos(freqs), jnp.sin(freqs))

        def _apply_rope(x, cos, sin):
            x1, x2 = jnp.split(x, 2, axis=-1)
            c = cos[None, None]
            s = sin[None, None]
            return jnp.concatenate([x1 * c - x2 * s, x1 * s + x2 * c], axis=-1)
        b, t, _ = x.shape
        cos, sin = _rope_tables(HEAD_DIM, ROPE_BASE, t)
        q = (x @ Wq).reshape(b, t, N_HEADS, HEAD_DIM).transpose(0, 2, 1, 3)
        k = (x @ Wk).reshape(b, t, N_KV, HEAD_DIM).transpose(0, 2, 1, 3)
        v = (x @ Wv).reshape(b, t, N_KV, HEAD_DIM).transpose(0, 2, 1, 3)
        q = _apply_rope(q, cos, sin)
        k = _apply_rope(k, cos, sin)
        k_h = jnp.repeat(k, GROUP_SIZE, axis=1)
        v_h = jnp.repeat(v, GROUP_SIZE, axis=1)
        scores = jnp.einsum('bhqd,bhkd->bhqk', q, k_h) / math.sqrt(HEAD_DIM)
        causal = jnp.triu(jnp.ones((t, t), dtype=bool), k=1)
        scores = jnp.where(causal[None, None], jnp.finfo(scores.dtype).min, scores)
        attn = jax.nn.softmax(scores, axis=-1)
        ctx = jnp.einsum('bhqk,bhkd->bhqd', attn, v_h)
        ctx = ctx.transpose(0, 2, 1, 3).reshape(b, t, D_OUT)
        return ctx @ Wo

    def _L0_ffn_ref(x, weight):
        import jax, jax.numpy as jnp
        import numpy as np
        GROUP_SIZE = 128
        THRESHOLD = 0.5
        EPS = 1e-08

        def ternary_quantize_groupwise(w):
            out_f, in_f = w.shape
            num_groups = in_f // GROUP_SIZE
            g = w.reshape(out_f, num_groups, GROUP_SIZE)
            scale = jnp.maximum(jnp.mean(jnp.abs(g), axis=-1, keepdims=True), EPS)
            w_norm = g / scale
            q = jnp.where(w_norm > THRESHOLD, 1.0, jnp.where(w_norm < -THRESHOLD, -1.0, 0.0))
            return (q * scale).reshape(out_f, in_f)
        w_q = ternary_quantize_groupwise(weight)
        return jnp.einsum('bsd,od->bso', x, w_q)
    x = L0_attn_x
    xn = _layernorm(x, axis=-1)
    s = _L0_attn_ref(xn, L0_attn_Wq, L0_attn_Wk, L0_attn_Wv, L0_attn_Wo)
    g = _silu(_L0_ffn_ref(xn, L0_ffn_weight))
    x = x + s * g
    return x

_drawn_inputs = setup_inputs


def setup_inputs(seed=0):
    import zlib

    import numpy as np

    out = dict(_drawn_inputs(seed))
    spreads = {}
    factors = {}
    for name, (base, spread) in spreads.items():
        noise = np.random.default_rng([zlib.crc32(name.encode()), seed]).standard_normal(out[name].shape)
        drawn = base * np.exp(spread * noise) if base else spread * noise
        out[name] = jnp.asarray(drawn.astype(out[name].dtype))
    for name, factor in factors.items():
        out[name] = (out[name] * factor).astype(out[name].dtype)
    return out
```

```python
from contextlib import ExitStack

import numpy as np

import concourse.bass as bass
from concourse import mybir

F32 = mybir.dt.float32
BF16 = mybir.dt.bfloat16
ALU = mybir.AluOpType
ACT = mybir.ActivationFunctionType
AX = mybir.AxisListType

P = 128
D = 512
DC = D // P
T = 1024
NT = T // P
NH = 32
NG = 8
HG = NH // NG
HD = D // NH
HALF = HD // 2
QK = D + NG * HD
QKV = QK + NG * HD
QKH = NH + NG
NPROD = 6
KS = NPROD * HD
KM = KS + 3
QUANT = 128
NQ = D // QUANT
THRESHOLD = 0.5
SCALE_EPS = 1e-8
LN_EPS = 1e-5
SM_SCALE = 1.0 / float(np.sqrt(HD))
LOWEST = -3.0e38
ROPE_BASE = 500000.0

UNITS = NT * (NT + 1) // 2
SPAN = 512 // P

Q_SLOT = (0, 0, 0, 1, 1, 2)
K_SLOT = (0, 1, 2, 0, 1, 0)

TURN_BANKS = (0, 5)
PROJ_BANKS = (1, 3)
STACK_BANKS = (6, 7)
SCORE_BANKS = (0, 1, 2)
MAX_BANKS = (3, 4)
ACC_BANKS = (5, 6)
ROW_BANK = 7
MERGE_BANK = 3
OUT_BANKS = (4, 7)

PROBS = 4


def first_unit(s):
    return s * (s + 1) // 2


def max_chunks(s):
    return [(half, j) for half in range(s // SPAN + 1) for j in range(HG)]


def chunks_before(s):
    return sum(len(max_chunks(r)) for r in range(s))


CHUNKS = chunks_before(NT)


def attention_steps():
    lead = 14.0
    steps = []
    cost = {}
    for s in range(NT):
        for half, j in max_chunks(s):
            width = min(s + 1 - half * SPAN, SPAN) * P
            cost[s, half, j] = width / 0.96 + 70
    whole, at = sum(cost.values()), 0.0
    for (s, half, j), c in cost.items():
        steps.append((at / whole * UNITS - lead, "max", (s, half, j)))
        at += c
        if (half, j) == max_chunks(s)[-1]:
            steps.append((at / whole * UNITS - lead, "split", (s,)))
            steps.append((at / whole * UNITS - lead + 3.05, "row", (s,)))
    lag = 2.5
    for s in range(NT):
        for kt in range(s + 1):
            u = first_unit(s) + kt
            steps.append((u, "score", (s, kt)))
            steps.append((u + lag, "value", (s, kt)))
        steps.append((u + lag + 0.1, "drain", (s,)))
        steps.append((u + lag + 1.6, "turn", (s,)))
    first = first_unit(NT - 1)
    steps.append((first + SPAN - 1 + lag + 0.2 - UNITS, "load", (0,)))
    steps.append((UNITS - 1 + lag + 0.2 - UNITS, "load", (1,)))
    return sorted(steps, key=lambda x: x[0])


STEPS = attention_steps()


def steps_within(start, stop, spans):
    found = [(time + UNITS * dg, dg, kind, args) for dg in spans for time, kind, args in STEPS
             if start <= time + UNITS * dg < stop]
    return [x[1:] for x in sorted(found, key=lambda x: x[0])]


PROLOGUE = steps_within(-UNITS, 0, (0,))
FIRST_BODY = steps_within(0, UNITS, (0, 1))
BODY = steps_within(0, UNITS, (-1, 0, 1))
LAST_BODY = steps_within(0, UNITS, (-1, 0))
EPILOGUE = steps_within(UNITS, 2 * UNITS, (0,))


def attention(eng, steps):
    def walk(plan, g):
        for dg, kind, args in plan:
            if kind in steps:
                steps[kind](g + dg, *args)

    walk(FIRST_BODY, 0)
    with eng.Fori(1, NG - 1) as g:
        walk(BODY, g)
    walk(LAST_BODY, NG - 1)
    walk(EPILOGUE, NG - 1)


def prologue(steps, linear=None):
    for i, (_, kind, args) in enumerate(PROLOGUE):
        for n in range(DC):
            if linear and i == len(PROLOGUE) * n // DC:
                linear(NT - DC + n)
        if kind in steps:
            steps[kind](0, *args)


def wait(eng, sem, value):
    if not isinstance(value, int) or value > 0:
        eng.wait_ge(sem, value)


def pass_waits(eng, sem):
    eng.sem_inc(sem, 1)


def build(nc, x, wq, wk, wv, wo, weight, rope_cos, rope_sin, out):
    with ExitStack() as ctx:
        def sb(name, shape, dt=F32):
            return ctx.enter_context(nc.sbuf_tensor(name, shape, dt))

        def sem(name):
            return ctx.enter_context(nc.semaphore(name))

        x_sb = sb("x_sb", [P, NT, D])
        xn = sb("xn", [P, 2, D])
        xnT = sb("xnT", [P, DC, T])
        w_qkv = sb("w_qkv", [P, DC, QKV])
        w_lin = sb("w_lin", [P, DC, D])
        w_linT = sb("w_linT", [P, DC, D])
        w_out = w_linT
        cos_sb = sb("cos_sb", [P, NT, HD])
        sin_sb = sb("sin_sb", [P, NT, HD])
        gate = sb("gate", [P, NT, D])
        qst = sb("qst", [KM, NG * NT * HG * P], BF16)
        kst = sb("kst", [KM, NG * T], BF16)
        v_all = sb("v_all", [P, NG * NT * HD])
        v_grp = sb("v_grp", [P, NT, 2 * HD])
        ident = sb("ident", [P, P])
        ident_b = sb("ident_b", [P, P], BF16)
        causal = sb("causal", [P, SPAN * P])
        stats = sb("stats", [P, NT, 6])
        mean_var = sb("mean_var", [P, NT, 2])
        var_eps = sb("var_eps", [P, NT])
        std = sb("std", [P, NT])
        rstd = sb("rstd", [P, NT])
        q_sum = sb("q_sum", [P, DC * NQ])
        q_scale = sb("q_scale", [P, DC * NQ])
        q_above = sb("q_above", [P, DC * NQ])
        q_below = sb("q_below", [P, DC * NQ])
        w_pos = sb("w_pos", [P, D])
        w_neg = sb("w_neg", [P, D])
        rope_a = sb("rope_a", [P, QK])
        rope_b = sb("rope_b", [P, QK])
        roped = sb("roped", [P, QK])
        rest = sb("rest", [P, QK])
        parts = sb("parts", [P, 2, QKH, NPROD, HD], BF16)
        z_exp = sb("z_exp", [P, D])
        z_den = sb("z_den", [P, D])
        top = sb("top", [P, 2, 2, HG])
        top_rest = sb("top_rest", [P, 2, HG])
        top_parts = sb("top_parts", [P, 2, HG, 3], BF16)
        seen = xn
        probs = w_lin
        drained = sb("drained", [P, 2, P])
        rden = sb("rden", [P, 2, HG])
        attn = xnT[:, :, :].rearrange("p c t -> p (c t)")
        attnT = w_qkv[:, 0:2, 0:D]
        gated = w_qkv[:, 2:4, 0:D]

        bank = ctx.enter_context(nc.psum_tensor("bank", [P, 8, 512], F32))
        banks_flat = bank[:, :, :].rearrange("p b n -> p (b n)")

        x_in = [sem(f"x_in{t}") for t in range(NT)]
        wqkv_in, wout_in, wlin_in, rope_in, out_done = map(sem, ("wqkv_in", "wout_in", "wlin_in", "rope_in", "out_done"))
        zeroed, ident_ready, causal_ready, ones_ready = map(sem, ("zeroed", "ident_ready", "causal_ready", "ones_ready"))
        stats_done, mean_done, eps_done, std_done, rstd_done, xn_done = map(
            sem, ("stats_done", "mean_done", "eps_done", "std_done", "rstd_done", "xn_done"))
        quant_step, signs_done, quant_done = map(sem, ("quant_step", "signs_done", "quant_done"))
        turned, turn_copied, qkv_done = map(sem, ("turned", "turn_copied", "qkv_done"))
        rope_done, roped_done, high_done, rest_done, mid_done, low_done = map(
            sem, ("rope_done", "roped_done", "high_done", "rest_done", "mid_done", "low_done"))
        stacked, stack_out_a, stack_out_v = map(sem, ("stacked", "stack_out_a", "stack_out_v"))
        z_done, zexp_done, zden_done, zrec_done, gate_done = map(
            sem, ("z_done", "zexp_done", "zden_done", "zrec_done", "gate_done"))
        max_scored, max_taken, split_step, row_turned, row_placed = map(
            sem, ("max_scored", "max_taken", "split_step", "row_turned", "row_placed"))
        v_loaded, scored, exp_done, masked, valued, acc_drained, acc_turned, rden_done, divided = map(
            sem, ("v_loaded", "scored", "exp_done", "masked", "valued", "acc_drained", "acc_turned", "rden_done", "divided"))
        pool_passed, dve_passed = sem("pool_passed"), sem("dve_passed")
        merged, merge_copied, projected, gated_done, summed = map(
            sem, ("merged", "merge_copied", "projected", "gated_done", "summed"))

        def q_rows(p0, p1, g, s, j=0, n=HG):
            return qst[p0:p1, bass.ds(g * (NT * HG * P) + (s * HG + j) * P, n * P)]

        def k_rows(p1, g, kt, n=1):
            return kst[0:p1, bass.ds(g * T + kt * P, n * P)]

        def tile_no(g, s):
            return g * NT + s

        def unit_no(g, s, kt):
            return g * UNITS + first_unit(s) + kt

        def chunk_no(g, s, half, j):
            return g * CHUNKS + chunks_before(s) + half * HG + j

        def heads(ap):
            return ap.rearrange("p (h d) -> p h d", d=HD)

        def z_bank(t):
            return TURN_BANKS[t % 2]

        def stack_src(n, b):
            flat = bank[0:KS, STACK_BANKS[n % 2], :].bitcast(BF16)
            return flat.rearrange("p (g n) -> p g n", g=2 if b < NH // 8 else NG)

        def stack_dst(t, b):
            if b < NH // 8:
                return qst[0:KS, :].rearrange("p (g t n) -> p g t n", g=NG, t=NT)[:, 2 * b:2 * b + 2, t, :]
            return kst[0:KS, :].rearrange("p (g t n) -> p g t n", g=NG, t=NT)[:, :, t, :]

        block = ctx.enter_context(nc.Block())

        @block.sync
        def _(sp):
            x_rows = x.rearrange("a (t p) d -> p (a t) d", p=P)
            for t in range(2):
                sp.dma_start(x_sb[:, t, :], x_rows[:, t, :]).then_inc(x_in[t], 16)
            sp.dma_start(w_qkv[:, :, 0:D], wq.rearrange("(c p) n -> p c n", p=P)).then_inc(wqkv_in, 16)
            sp.dma_start(w_lin[:, :, :], weight.rearrange("(c p) n -> p c n", p=P)).then_inc(wlin_in, 16)
            for t in range(2, NT):
                sp.dma_start(x_sb[:, t, :], x_rows[:, t, :]).then_inc(x_in[t], 16)
            sp.wait_ge(z_done, NT)
            sp.dma_start(w_out[:, :, :], wo.rearrange("(c p) n -> p c n", p=P)).then_inc(wout_in, 16)
            out_rows = out.rearrange("a (t p) d -> p (a t) d", p=P)
            for t in range(NT):
                sp.wait_ge(summed, t + 1)
                sp.dma_start(out_rows[:, t, :], x_sb[:, t, :]).then_inc(out_done, 16)
            sp.wait_ge(out_done, 16 * NT)

        @block.gpsimd
        def _(pool):
            pool.memset(v_grp[:, :, HD:2 * HD], 1.0).then_inc(ones_ready, 1)
            for m in (ident, ident_b, causal):
                pool.memset(m[:, :], 0.0).then_inc(zeroed, 1)
            pool.wait_ge(zeroed, 3)
            for m in (ident, ident_b):
                pool.affine_select(out=m[:, :], in_=m[:, :], compare_op=ALU.not_equal, fill=1.0, base=0,
                                   pattern=[[-1, P]], channel_multiplier=1).then_inc(ident_ready, 1)
            last_tile = causal[:, (SPAN - 1) * P:SPAN * P]
            pool.affine_select(out=last_tile, in_=last_tile, compare_op=ALU.is_ge, fill=LOWEST, base=0,
                               pattern=[[-1, P]], channel_multiplier=1).then_inc(causal_ready, 1)
            pool.wait_ge(causal_ready, 1)
            pool.memset(kst[KS:KM, :], 1.0).then_inc(ones_ready, 1)
            pool.wait_ge(ones_ready, 2)

            def quantise(c):
                pool.wait_ge(signs_done, c + 1)
                pool.tensor_tensor(w_lin[:, c, :], w_pos[:, :], w_neg[:, :], ALU.subtract).then_inc(quant_done, 1)

            quantise(0)
            for t in range(NT):
                pool.wait_ge(rope_done, t + 1)
                if t >= 1:
                    pool.wait_ge(high_done, t)
                pool.tensor_tensor(roped[:, :], rope_a[:, :], rope_b[:, :], ALU.add).then_inc(roped_done, 1)
                if t + 1 < DC:
                    quantise(t + 1)
                pool.wait_ge(mid_done, t + 1)
                stk = parts[:, t % 2]
                pool.tensor_tensor(stk[:, 0:NH, 5, :], heads(rest[:, 0:D]), stk[:, 0:NH, 3, :], ALU.subtract)
                pool.tensor_tensor(stk[:, NH:QKH, 2, :], heads(rest[:, D:QK]), stk[:, NH:QKH, 1, :],
                                   ALU.subtract).then_inc(low_done, 1)

            def split(g, s):
                n = tile_no(g, s)
                pool.wait_ge(max_taken, chunk_no(g, s, *max_chunks(s)[-1]) + 1)
                wait(pool, row_turned, n - 1)
                pass_waits(pool, pool_passed)
                t0, t1 = top[:, s % 2, s // SPAN, :], top_rest[:, s % 2, :]
                part = [top_parts[:, s % 2, :, i] for i in range(3)]
                pool.tensor_scalar(part[0], t0, -1.0, None, ALU.mult).then_inc(split_step, 1)
                pool.wait_ge(split_step, n * 5 + 1)
                pool.tensor_tensor(t1, t0, part[0], ALU.add).then_inc(split_step, 1)
                pool.wait_ge(split_step, n * 5 + 2)
                pass_waits(pool, pool_passed)
                pool.tensor_scalar(part[1], t1, -1.0, None, ALU.mult).then_inc(split_step, 1)
                pool.wait_ge(split_step, n * 5 + 3)
                pool.tensor_tensor(t1, t1, part[1], ALU.add).then_inc(split_step, 1)
                pool.wait_ge(split_step, n * 5 + 4)
                pass_waits(pool, pool_passed)
                pool.tensor_scalar(part[2], t1, -1.0, None, ALU.mult).then_inc(split_step, 1)

            def load(g, half):
                before = first_unit(NT - 1) + SPAN if half == 0 else UNITS
                wait(pool, valued, (g - 1) * UNITS + before)
                n = SPAN * HD
                pool.tensor_copy(v_grp[:, half * SPAN:(half + 1) * SPAN, 0:HD],
                                 heads(v_all[:, bass.ds(g * (2 * n) + half * n, n)])).then_inc(v_loaded, 1)

            def mask(g, s, kt):
                if kt < s:
                    return
                u = unit_no(g, s, kt)
                pool.wait_ge(exp_done, u + 1)
                pass_waits(pool, pool_passed)
                p = probs[:, (first_unit(s) + kt) % PROBS, :].rearrange("p (h q) -> p h q", h=HG)
                pool.affine_select(out=p, in_=p, compare_op=ALU.is_ge, fill=0.0, base=0,
                                   pattern=[[0, HG], [1, P]], channel_multiplier=-1).then_inc(masked, 1)

            steps = {"split": split, "load": load, "score": mask}
            pool.wait_ge(rope_done, NT)
            prologue(steps)
            attention(pool, steps)

        @block.scalar
        def _(act):
            for w, lo, hi in ((wk, D, QK), (wv, QK, QKV)):
                act.dma_start(w_qkv[:, :, lo:hi], w.rearrange("(c p) n -> p c n", p=P)).then_inc(wqkv_in, 16)
            for sbuf, dram in ((cos_sb, rope_cos), (sin_sb, rope_sin)):
                act.dma_start(sbuf[:, :, :], dram).then_inc(rope_in, 16)

            def deviation(t):
                act.wait_ge(eps_done, t + 1)
                act.activation(std[:, t:t + 1], var_eps[:, t:t + 1], ACT.Sqrt).then_inc(std_done, 1)

            turn_count = 0

            def turn_out(dst):
                nonlocal turn_count
                act.wait_ge(turned, turn_count + 1)
                src = bank[:, TURN_BANKS[turn_count % 2], :].rearrange("p (c n) -> p c n", c=DC)
                act.activation(dst, src, ACT.Copy).then_inc(turn_copied, 1)
                turn_count += 1

            def x_out(t):
                turn_out(xnT[:, :, t * P:(t + 1) * P])

            def high(t):
                act.wait_ge(roped_done, t + 1)
                if t >= 2:
                    act.wait_ge(stacked, QKH // 8 * (t - 1))
                stk = parts[:, t % 2]
                q, k = heads(roped[:, 0:D]).unsqueeze(2), heads(roped[:, D:QK]).unsqueeze(2)
                act.activation(stk[:, 0:NH, 0:3, :], q.broadcast_to([P, NH, 3, HD]), ACT.Copy)
                act.activation(stk[:, NH:QKH, 0:4:3, :], k.broadcast_to([P, NG, 2, HD]), ACT.Copy)
                act.activation(stk[:, NH:QKH, 5:6, :], k, ACT.Copy).then_inc(high_done, 1)

            def stack_out(t):
                for b in range(QKH // 8):
                    n = t * (QKH // 8) + b
                    if n % 2 == 0:
                        act.wait_ge(stacked, n + 1)
                        act.activation(stack_dst(t, b), stack_src(n, b), ACT.Copy).then_inc(stack_out_a, 1)

            def z_exponential(t):
                act.wait_ge(z_done, t + 1)
                if t >= 1:
                    act.wait_ge(zden_done, t)
                act.activation(z_exp[:, :], bank[:, z_bank(t), :], ACT.Exp, scale=-1.0).then_inc(zexp_done, 1)

            deviation(0)
            deviation(1)
            x_out(0)
            x_out(1)
            for t in range(NT):
                if t < NT // 2 - 1:
                    deviation(2 * t + 2)
                    deviation(2 * t + 3)
                    x_out(2 * t + 2)
                    x_out(2 * t + 3)
                high(t)
                if t < DC:
                    turn_out(w_linT[:, :, t * P:(t + 1) * P])
                else:
                    z_exponential(t - DC)
                if t >= 1:
                    stack_out(t - 1)
            stack_out(NT - 1)

            def exponential(g, s, kt):
                u = unit_no(g, s, kt)
                k = first_unit(s) + kt
                act.wait_ge(scored, u + 1)
                wait(act, valued, u + 1 - PROBS)
                act.activation(probs[:, k % PROBS, :], bank[:, SCORE_BANKS[k % 3], :], ACT.Exp,
                               scale=SM_SCALE).then_inc(exp_done, 1)

            def place_rows(g, s):
                act.wait_ge(row_turned, tile_no(g, s) + 1)
                act.activation(q_rows(KS, KM, g, s), bank[KS:KM, ROW_BANK, 0:HG * P // 2].bitcast(BF16),
                               ACT.Copy).then_inc(row_placed, 1)

            def drain(g, s):
                n = tile_no(g, s)
                act.wait_ge(valued, unit_no(g, s, s) + 1)
                wait(act, acc_turned, n - 1)
                act.activation(drained[:, s % 2, :], bank[:, ACC_BANKS[s % 2], 0:P], ACT.Copy).then_inc(acc_drained, 1)

            steps = {"score": exponential, "row": place_rows, "drain": drain}
            prologue(steps, z_exponential)
            attention(act, steps)
            for t in range(NT):
                act.wait_ge(merged, t + 1)
                if t >= 2:
                    act.wait_ge(projected, t - 1)
                act.activation(attnT[:, t % 2, :], bank[:, MERGE_BANK, :], ACT.Copy).then_inc(merge_copied, 1)

        @block.vector
        def _(dve):
            def normalise(t):
                dve.wait_ge(x_in[t], 16)
                dve.bn_stats(stats[:, t, :], x_sb[:, t, :]).then_inc(stats_done, 1)
                dve.wait_ge(stats_done, t + 1)
                dve.bn_aggr(mean_var[:, t, :], stats[:, t, :]).then_inc(mean_done, 1)
                dve.wait_ge(mean_done, t + 1)
                dve.tensor_scalar(var_eps[:, t:t + 1], mean_var[:, t, 1:2], LN_EPS, None, ALU.add).then_inc(eps_done, 1)
                dve.wait_ge(std_done, t + 1)
                dve.reciprocal(rstd[:, t:t + 1], std[:, t:t + 1]).then_inc(rstd_done, 1)
                dve.wait_ge(rstd_done, t + 1)
                if t >= 2:
                    dve.wait_ge(turned, x_turns_before(t - 2) + 1)
                dve.tensor_scalar(xn[:, t % 2, :], x_sb[:, t, :], mean_var[:, t, 0:1], rstd[:, t:t + 1],
                                  ALU.subtract, ALU.mult).then_inc(xn_done, 1)

            def quantise(c):
                if c >= 1:
                    dve.wait_ge(quant_done, c)
                for i in range(NQ):
                    n, cols = c * NQ + i, slice(i * QUANT, (i + 1) * QUANT)
                    dve.tensor_scalar(w_pos[:, cols], w_lin[:, c, cols], q_above[:, n:n + 1], q_scale[:, n:n + 1],
                                      ALU.is_gt, ALU.mult)
                    last = dve.tensor_scalar(w_neg[:, cols], w_lin[:, c, cols], q_below[:, n:n + 1],
                                             q_scale[:, n:n + 1], ALU.is_lt, ALU.mult)
                last.then_inc(signs_done, 1)

            normalise(0)
            normalise(1)
            dve.wait_ge(wlin_in, 16)
            dve.tensor_reduce(q_sum[:, :], w_lin[:, :, :].rearrange("p c (n k) -> p (c n) k", k=QUANT), AX.X, ALU.add,
                              apply_absolute_value=True).then_inc(quant_step, 1)
            dve.wait_ge(quant_step, 1)
            dve.tensor_scalar(q_scale[:, :], q_sum[:, :], 1.0 / QUANT, SCALE_EPS, ALU.mult, ALU.max).then_inc(quant_step, 1)
            dve.wait_ge(quant_step, 2)
            dve.tensor_scalar(q_above[:, :], q_scale[:, :], THRESHOLD, None, ALU.mult).then_inc(quant_step, 1)
            dve.tensor_scalar(q_below[:, :], q_scale[:, :], -THRESHOLD, None, ALU.mult).then_inc(quant_step, 1)
            dve.wait_ge(quant_step, 4)
            quantise(0)

            def rotate(t):
                dve.wait_ge(qkv_done, t + 1)
                b = PROJ_BANKS[t % 2] * 512
                qk = heads(banks_flat[:, b:b + QK])
                a, r = heads(rope_a[:, :]), heads(rope_b[:, :])

                def over_heads(table, lo, hi):
                    return table[:, t, lo:hi].unsqueeze(1).broadcast_to([P, QKH, hi - lo])

                dve.tensor_tensor(a, qk, over_heads(cos_sb, 0, HD), ALU.mult)
                dve.tensor_tensor(r[:, :, 0:HALF], qk[:, :, HALF:HD], over_heads(sin_sb, 0, HALF), ALU.mult)
                dve.tensor_tensor(r[:, :, HALF:HD], qk[:, :, 0:HALF], over_heads(sin_sb, HALF, HD), ALU.mult)
                v = v_all[:, :].rearrange("p (g t d) -> p g t d", g=NG, t=NT)[:, :, t, 0:HD]
                dve.tensor_copy(v, heads(banks_flat[:, b + QK:b + QKV])).then_inc(rope_done, 1)

            def mid(t):
                dve.wait_ge(high_done, t + 1)
                if t >= 1:
                    dve.wait_ge(low_done, t)
                stk = parts[:, t % 2]
                dve.tensor_tensor(heads(rest[:, :]), heads(roped[:, :]), stk[:, :, 0, :], ALU.subtract).then_inc(rest_done, 1)
                dve.wait_ge(rest_done, t + 1)
                q, k = heads(rest[:, 0:D]).unsqueeze(2), heads(rest[:, D:QK]).unsqueeze(2)
                dve.tensor_copy(stk[:, 0:NH, 3:5, :], q.broadcast_to([P, NH, 2, HD]))
                dve.tensor_copy(stk[:, NH:QKH, 1:5:3, :], k.broadcast_to([P, NG, 2, HD])).then_inc(mid_done, 1)

            def stack_out(t):
                for b in range(QKH // 8):
                    n = t * (QKH // 8) + b
                    if n % 2 == 1:
                        dve.wait_ge(stacked, n + 1)
                        dve.tensor_copy(stack_dst(t, b), stack_src(n, b)).then_inc(stack_out_v, 1)

            def gating(t):
                dve.wait_ge(zexp_done, t + 1)
                dve.tensor_scalar(z_den[:, :], z_exp[:, :], 1.0, None, ALU.add).then_inc(zden_done, 1)
                dve.wait_ge(zden_done, t + 1)
                dve.reciprocal(z_den[:, :], z_den[:, :]).then_inc(zrec_done, 1)
                dve.wait_ge(zrec_done, t + 1)
                dve.tensor_tensor(gate[:, t, :], bank[:, z_bank(t), :], z_den[:, :], ALU.mult).then_inc(gate_done, 1)

            dve.wait_ge(rope_in, 32)
            for t in range(NT):
                if t < NT // 2 - 1:
                    normalise(2 * t + 2)
                    normalise(2 * t + 3)
                rotate(t)
                if t + 1 < DC:
                    quantise(t + 1)
                if t >= 1:
                    stack_out(t - 1)
                mid(t)
                if t >= DC:
                    gating(t - DC)
            stack_out(NT - 1)

            def maximum(g, s, half, j):
                n, c = tile_no(g, s), chunk_no(g, s, half, j)
                dve.wait_ge(max_scored, c + 1)
                if (half, j) == (0, 0):
                    wait(dve, split_step, (n - 1) * 5)
                b = MAX_BANKS[(chunks_before(s) + half * HG + j) % 2]
                tiles = s + 1 - half * SPAN
                to = top[:, s % 2, half, j:j + 1]
                if tiles > SPAN:
                    dve.tensor_reduce(to, bank[:, b, :], AX.X, ALU.max).then_inc(max_taken, 1)
                    return
                start = LOWEST
                if half:
                    dve.wait_ge(max_taken, chunk_no(g, s, 0, j) + 1)
                    start = top[:, s % 2, 0, j:j + 1]
                pass_waits(dve, dve_passed)
                w = tiles * P
                dve.tensor_tensor_reduce(seen[:, b % 2, 0:w], bank[:, b, 0:w], causal[:, SPAN * P - w:], 1.0, start,
                                         ALU.add, ALU.max, to).then_inc(max_taken, 1)

            def divide(g, s):
                n = tile_no(g, s)
                dve.wait_ge(acc_turned, n + 1)
                res = bank[:, ACC_BANKS[s % 2], P:2 * P].rearrange("p (h d) -> p h d", h=HG)
                r = rden[:, s % 2, :]
                dve.reciprocal(r, res[:, :, HD]).then_inc(rden_done, 1)
                dve.wait_ge(rden_done, n + 1)
                to = attn[:, bass.ds(g * (HG * HD) + s * D, HG * HD)]
                dve.tensor_tensor(heads(to), res[:, :, 0:HD], r.unsqueeze(2).broadcast_to([P, HG, HD]),
                                  ALU.mult).then_inc(divided, 1)

            dve.wait_ge(causal_ready, 1)
            steps = {"max": maximum, "turn": divide}
            prologue(steps, gating)
            attention(dve, steps)
            for t in range(NT):
                dve.wait_ge(projected, t + 1)
                dve.tensor_tensor(gated[:, t % 2, :], bank[:, OUT_BANKS[t % 2], :], gate[:, t, :], ALU.mult).then_inc(gated_done, 1)
                dve.wait_ge(gated_done, t + 1)
                dve.tensor_tensor(x_sb[:, t, :], gated[:, t % 2, :], x_sb[:, t, :], ALU.add).then_inc(summed, 1)

        @block.tensor
        def _(pe):
            turn_count = 0

            def turn(src):
                nonlocal turn_count
                wait(pe, turn_copied, turn_count - 1)
                for c in range(DC):
                    last = pe.transpose(bank[:, TURN_BANKS[turn_count % 2], c * P:(c + 1) * P],
                                        src[:, c * P:(c + 1) * P], ident[:, :])
                last.then_inc(turned, 1)
                turn_count += 1

            def x_turn(t):
                pe.wait_ge(xn_done, t + 1)
                turn(xn[:, t % 2, :])

            def project(t):
                pe.wait_ge(turn_copied, x_turns_before(t) + 1)
                if t >= 2:
                    pe.wait_ge(rope_done, t - 1)
                b = PROJ_BANKS[t % 2]
                for lo, hi, dst in ((0, D, b), (D, QKV, b + 1)):
                    for c in range(DC):
                        last = pe.matmul(bank[:, dst, 0:hi - lo], xnT[:, c, t * P:(t + 1) * P], w_qkv[:, c, lo:hi],
                                         start=(c == 0), stop=(c == DC - 1))
                last.then_inc(qkv_done, 1)

            def linear(t):
                if t == 0:
                    pe.wait_ge(turn_copied, turn_count)
                if t >= 2:
                    pe.wait_ge(gate_done, t - 1)
                for c in range(DC):
                    last = pe.matmul(bank[:, z_bank(t), :], xnT[:, c, t * P:(t + 1) * P], w_linT[:, c, :],
                                     start=(c == 0), stop=(c == DC - 1))
                last.then_inc(z_done, 1)

            def stack(t):
                pe.wait_ge(low_done, t + 1)
                pe.wait_ge(mid_done, t + 1)
                pe.wait_ge(high_done, t + 1)
                for b in range(QKH // 8):
                    n = t * (QKH // 8) + b
                    wait(pe, stack_out_v if n % 2 else stack_out_a, n // 2)
                    dst = bank[0:KS, STACK_BANKS[n % 2], :].bitcast(BF16)
                    for i in range(8):
                        last = pe.transpose(dst[:, i * P:(i + 1) * P],
                                            parts[:, t % 2, 8 * b + i].rearrange("p n d -> p (n d)"), ident_b[:, :])
                    last.then_inc(stacked, 1)

            pe.wait_ge(ident_ready, 2)
            x_turn(0)
            x_turn(1)
            pe.wait_ge(wqkv_in, 48)
            for t in range(NT):
                project(t)
                if t < NT // 2 - 1:
                    x_turn(2 * t + 2)
                    x_turn(2 * t + 3)
                if t < DC:
                    pe.wait_ge(quant_done, t + 1)
                    turn(w_lin[:, t, :])
                else:
                    linear(t - DC)
                if t >= 1:
                    stack(t - 1)
            stack(NT - 1)

            def score_for_max(g, s, half, j):
                c = chunks_before(s) + half * HG + j
                wait(pe, max_taken, chunk_no(g, s, half, j) - 1)
                n = min(s + 1 - half * SPAN, SPAN)
                pe.matmul(bank[:, MAX_BANKS[c % 2], 0:n * P], q_rows(0, KS, g, s, j, 1), k_rows(KS, g, half * SPAN, n),
                          start=True, stop=True).then_inc(max_scored, 1)

            def turn_rows(g, s):
                n = tile_no(g, s)
                pe.wait_ge(split_step, (n + 1) * 5)
                wait(pe, row_placed, n)
                dst = bank[KS:KM, ROW_BANK, 0:HG * P // 2].bitcast(BF16)
                for j in range(HG):
                    last = pe.transpose(dst[:, j * P:(j + 1) * P], top_parts[:, s % 2, j, :], ident_b[:, :])
                last.then_inc(row_turned, 1)

            def score(g, s, kt):
                u, k = unit_no(g, s, kt), first_unit(s) + kt
                if kt == 0:
                    pe.wait_ge(row_placed, tile_no(g, s) + 1)
                wait(pe, exp_done, u - 2)
                pe.matmul(bank[:, SCORE_BANKS[k % 3], :], k_rows(KM, g, kt), q_rows(0, KM, g, s),
                          start=True, stop=True).then_inc(scored, 1)

            def value(g, s, kt):
                u, k = unit_no(g, s, kt), first_unit(s) + kt
                if kt == 0:
                    wait(pe, divided, tile_no(g, s) - 1)
                if (s, kt) in ((0, 0), (SPAN, SPAN)):
                    pe.wait_ge(v_loaded, 2 * g + 1 + (s > 0))
                pe.wait_ge(exp_done, u + 1)
                if kt == s:
                    pe.wait_ge(masked, tile_no(g, s) + 1)
                for j in range(HG):
                    last = pe.matmul(bank[j * 2 * HD:(j + 1) * 2 * HD, ACC_BANKS[s % 2], 0:P], v_grp[:, kt, :],
                                     probs[:, k % PROBS, j * P:(j + 1) * P], start=(kt == 0), stop=(kt == s))
                last.then_inc(valued, 1)

            def turn_back(g, s):
                pe.wait_ge(acc_drained, tile_no(g, s) + 1)
                pe.transpose(bank[:, ACC_BANKS[s % 2], P:2 * P], drained[:, s % 2, :], ident[:, :]).then_inc(acc_turned, 1)

            steps = {"max": score_for_max, "row": turn_rows, "score": score, "value": value, "turn": turn_back}
            pe.wait_ge(stack_out_a, NT * (QKH // 8) // 2)
            pe.wait_ge(stack_out_v, NT * (QKH // 8) // 2)
            pe.wait_ge(ones_ready, 2)
            prologue(steps, linear)
            pe.wait_ge(gate_done, NT)
            attention(pe, steps)

            pe.wait_ge(wout_in, 16)

            def merge(t):
                pe.wait_ge(divided, tile_no(NG - 1, t) + 1)
                wait(pe, merge_copied, t)
                for c in range(DC):
                    last = pe.transpose(bank[:, MERGE_BANK, c * P:(c + 1) * P],
                                        attn[:, t * D + c * P:t * D + (c + 1) * P], ident[:, :])
                last.then_inc(merged, 1)

            merge(0)
            for t in range(NT):
                if t + 1 < NT:
                    merge(t + 1)
                pe.wait_ge(merge_copied, t + 1)
                wait(pe, gated_done, t - 1)
                for c in range(DC):
                    last = pe.matmul(bank[:, OUT_BANKS[t % 2], :], attnT[:, t % 2, c * P:(c + 1) * P], w_out[:, c, :],
                                     start=(c == 0), stop=(c == DC - 1))
                last.then_inc(projected, 1)


def x_turns_before(t):
    return t + max(0, t // 2 - 1)


def rope_tables():
    inv = (1.0 / ROPE_BASE ** (np.arange(0, HD, 2, dtype=np.float32) / np.float32(HD))).astype(np.float32)
    freqs = np.arange(T, dtype=np.float32)[:, None] * inv[None, :]
    cos, sin = np.cos(freqs).astype(np.float32), np.sin(freqs).astype(np.float32)

    def by_tile(a):
        return np.ascontiguousarray(a.reshape(NT, P, HD).transpose(1, 0, 2))
    return by_tile(np.concatenate([cos, cos], 1)), by_tile(np.concatenate([-sin, sin], 1))


_INS = ["L0_attn_x", "L0_attn_Wq", "L0_attn_Wk", "L0_attn_Wv", "L0_attn_Wo", "L0_ffn_weight"]


def kernel(**inputs):
    import concourse.bacc as bacc
    from concourse.bass_utils import run_bass_kernel_spmd

    nc = bacc.Bacc("TRN2", target_bir_lowering=False, num_devices=1)
    arrays = {name: np.ascontiguousarray(inputs[name]) for name in _INS}
    arrays["rope_cos"], arrays["rope_sin"] = rope_tables()
    args = [nc.dram_tensor(name, a.shape, mybir.dt.from_np(a.dtype), kind="ExternalInput").ap()
            for name, a in arrays.items()]
    out = nc.dram_tensor("out", (1, T, D), F32, kind="ExternalOutput").ap()
    build(nc, *args, out)
    got = run_bass_kernel_spmd(nc, [arrays], core_ids=[0])
    return got.results[0]["out"]
```

```python
from contextlib import ExitStack

import numpy as np

import concourse.bass as bass
from concourse import mybir

F32 = mybir.dt.float32
BF16 = mybir.dt.bfloat16
ALU = mybir.AluOpType
ACT = mybir.ActivationFunctionType
AX = mybir.AxisListType

P = 128
D = 512
DC = D // P
T = 1024
NT = T // P
NH = 32
NG = 8
HG = NH // NG
HD = D // NH
HALF = HD // 2
QK = D + NG * HD
QKV = QK + NG * HD
QKH = NH + NG
NPROD = 6
KS = NPROD * HD
KM = KS + 3
QUANT = 128
NQ = D // QUANT
THRESHOLD = 0.5
SCALE_EPS = 1e-8
LN_EPS = 1e-5
SM_SCALE = 1.0 / float(np.sqrt(HD))
LOWEST = -3.0e38
ROPE_BASE = 500000.0

SPAN = 512 // P
NB = NT // SPAN

Q_SLOT = (0, 0, 0, 1, 1, 2)
K_SLOT = (0, 1, 2, 0, 1, 0)

TURN_BANKS = (0, 5)
EARLY_BANK = 0
Z_BANKS = (5, 1)
PROJ_BANKS = (1, 3)
STACK_BANKS = (6, 7)
SCORE_BANKS = (0, 1, 2)
MAX_BANKS = (3, 4, 7)
ACC_BANK = 5
SMALL_BANK = 6
MERGE_BANK = 3
OUT_BANKS = (4, 7)

PROBS = 3


PAIRS = [(b, kt) for b in range(NB) for kt in range(SPAN * (b + 1))]


def queries(b, kt):
    return min(SPAN, SPAN * (b + 1) - kt) * P


FIXED = 0.1
SCORE_TIME = [queries(*pair) / 512 + FIXED for pair in PAIRS for _ in range(HG)]
GROUP_TIME = sum(SCORE_TIME)
BLOCK_START = [sum(SCORE_TIME[:PAIRS.index((b, 0)) * HG]) for b in range(NB)]
SLACK, ROW_LAG, VALUE_LAG, DRAIN_LAG, TURN_LAG = 1.0, 3.03, 4, 0.03, 4.5
LEAD = GROUP_TIME - BLOCK_START[-1] + ROW_LAG + SLACK


def score_start(i):
    again, i = divmod(i, len(SCORE_TIME))
    return again * GROUP_TIME + sum(SCORE_TIME[:i])


def max_chunks(s):
    return [(half, j) for half in range(s // SPAN + 1) for j in range(HG)]


def chunks_before(s):
    return sum(len(max_chunks(r)) for r in range(s))


CHUNKS = chunks_before(NT)


def attention_steps():
    steps = []
    cost = {(s, half, j): min(s + 1 - half * SPAN, SPAN) * P / 0.96 + 70
            for s in range(NT) for half, j in max_chunks(s)}
    whole, at = sum(cost.values()), 0.0
    for (s, half, j), c in cost.items():
        steps.append((at / whole * GROUP_TIME - LEAD, "max", (s, half, j)))
        at += c
        if (half, j) == max_chunks(s)[-1]:
            steps.append((at / whole * GROUP_TIME - LEAD, "split", (s,)))
            steps.append((at / whole * GROUP_TIME - LEAD + ROW_LAG, "row", (s,)))
    for n, (b, kt) in enumerate(PAIRS):
        for j in range(HG):
            steps.append((score_start(n * HG + j), "score", (b, kt, j)))
        if kt >= SPAN * b:
            steps.append((score_start((n + 1) * HG) - 0.01, "mask", (b, kt)))
        at = score_start((n + 1) * HG + VALUE_LAG) - 0.01
        steps.append((at, "value", (b, kt)))
        if kt == SPAN * (b + 1) - 1:
            steps.append((at + DRAIN_LAG, "drain", (b,)))
            steps.append((at + DRAIN_LAG + TURN_LAG, "turn", (b,)))
        if b == NB - 1 and kt % SPAN == SPAN - 1:
            steps.append((at + 0.02 - GROUP_TIME, "load", (kt // SPAN,)))
    return sorted(steps, key=lambda x: x[0])


STEPS = attention_steps()


def steps_within(start, stop, spans, more=()):
    found = [(time + GROUP_TIME * dg, dg, kind, args) for dg in spans for time, kind, args in STEPS
             if start <= time + GROUP_TIME * dg < stop]
    found += [(time, 0, kind, args) for time, kind, args in more if start <= time < stop]
    return [x[1:] for x in sorted(found, key=lambda x: x[0])]


def time_of(kind, s):
    return next(time for time, k, args in STEPS if k == kind and args == (s,))


TAIL_STEP, TAIL_LAG = (5.0, 1.0), 1.3
TAIL = []
for _t in range(NT):
    _at = time_of("turn", _t // SPAN) + 0.3 + _t % SPAN * TAIL_STEP[_t // SPAN]
    TAIL += [(_at, "merge", (_t,)), (_at + TAIL_LAG, "finish", (_t,))]

EARLY_HALVES = ((0, 0), (1, 0), (2, 0), (3, 0), (4, 0), (4, 1), (5, 0), (5, 1), (6, 0))
WITH_PROJECTION = {4: 0, 5: 2, 7: 5}
WITH_LINEAR = {0: 1, 1: 3, 2: 4, 3: 6, 4: 7, 5: 8}


def complete(half):
    return half[0] // SPAN == half[1]


def early_portion(n):
    s, half = EARLY_HALVES[n]
    turned = n >= 2 and complete(EARLY_HALVES[n - 2])
    slots = [[("row", (EARLY_HALVES[n - 2][0],))] if turned else []]
    slots += [[("max", (s, half, j))] for j in range(HG)]
    if complete((s, half)):
        slots[-1].append(("split", (s,)))
    return slots


EARLY = [early_portion(n) for n in range(len(EARLY_HALVES))]
EARLY_STEPS = [step for portion in EARLY for slot in portion for step in slot]
PROLOGUE = [x for x in steps_within(-GROUP_TIME, 0, (0,)) if x[1:] not in EARLY_STEPS]
FIRST_BODY = steps_within(0, GROUP_TIME, (0, 1))
BODY = steps_within(0, GROUP_TIME, (-1, 0, 1))
LAST_BODY = steps_within(0, GROUP_TIME, (-1, 0), TAIL)
EPILOGUE = steps_within(GROUP_TIME, 2 * GROUP_TIME, (0,), TAIL)


def issued_before(kind, at, per_group):
    return sum(time + GROUP_TIME * dg < at for dg in (-1, 0, 1) for time, k, _ in STEPS if k == kind) - per_group


def attention(eng, steps):
    def walk(plan, g):
        for dg, kind, args in plan:
            if kind in steps:
                steps[kind](g + dg, *args)

    walk(FIRST_BODY, 0)
    with eng.Fori(1, NG - 1) as g:
        walk(BODY, g)
    walk(LAST_BODY, NG - 1)
    walk(EPILOGUE, NG - 1)


def early(steps, portion, slots=range(HG + 1)):
    if portion is not None:
        for slot in slots:
            for kind, args in EARLY[portion][slot]:
                if kind in steps:
                    steps[kind](0, *args, early=True)


def prologue(steps, linear=None):
    for i, (_, kind, args) in enumerate(PROLOGUE):
        if linear and i in (0, len(PROLOGUE) // 2):
            linear(NT - 2 + (i > 0))
        if kind in steps:
            steps[kind](0, *args)


def wait(eng, sem, value):
    if not isinstance(value, int) or value > 0:
        eng.wait_ge(sem, value)


def pass_waits(eng, sem):
    eng.sem_inc(sem, 1)


def attn_block(ap):
    return bass.AP(ap.tensor, ap.offset, [ap.ap[0], [D, SPAN], [HD, HG], [1, HD]])


def build(nc, x, wq, wk, wv, wo, weight, rope_cos, rope_sin, out):
    with ExitStack() as ctx:
        def sb(name, shape, dt=F32):
            return ctx.enter_context(nc.sbuf_tensor(name, shape, dt))

        def sem(name):
            return ctx.enter_context(nc.semaphore(name))

        x_sb = sb("x_sb", [P, NT, D])
        xn = sb("xn", [P, 2, D])
        xnT = sb("xnT", [P, DC, T])
        w_qkv = sb("w_qkv", [P, DC, QKV])
        probs = sb("probs", [P, PROBS, HG, 512])
        room = probs[:, :, :, :].rearrange("p b h n -> p (b h n)")
        sizes = (DC * D, D, D, QK, QK, QK, QK)
        starts = [sum(sizes[:i]) for i in range(len(sizes))]
        w_lin, w_pos, w_neg, rope_a, rope_b, roped, rest = [room[:, a:a + n] for a, n in zip(starts, sizes)]
        w_lin = w_lin.rearrange("p (c d) -> p c d", c=DC)
        w_linT = sb("w_linT", [P, DC, D])
        w_out = w_linT
        cos_sb = sb("cos_sb", [P, NT, HD])
        sin_sb = sb("sin_sb", [P, NT, HD])
        gate = sb("gate", [P, NT, D])
        qst = sb("qst", [KM, NH * T], BF16)
        kst = sb("kst", [KM, NG * T], BF16)
        v_all = sb("v_all", [P, NG * NT * HD])
        v_grp = sb("v_grp", [P, NT, 2 * HD])
        ident = sb("ident", [P, P])
        ident_b = sb("ident_b", [P, P], BF16)
        causal = sb("causal", [P, SPAN * P])
        stats = sb("stats", [P, NT, 6])
        mean_var = sb("mean_var", [P, NT, 2])
        var_eps = sb("var_eps", [P, NT])
        std = sb("std", [P, NT])
        rstd = sb("rstd", [P, NT])
        q_sum = sb("q_sum", [P, DC * NQ])
        q_scale = sb("q_scale", [P, DC * NQ])
        q_above = sb("q_above", [P, DC * NQ])
        q_below = sb("q_below", [P, DC * NQ])
        parts = sb("parts", [P, 2, QKH, NPROD, HD], BF16)
        seen_early = sb("seen_early", [P, 512])
        tanh_z = sb("tanh_z", [P, 2, D])
        top = sb("top", [P, 2, 2, HG])
        top_rest = sb("top_rest", [P, 2, HG])
        top_parts = sb("top_parts", [P, 2, HG, 3], BF16)
        seen = w_qkv[:, 0:3, 0:D]
        drained = w_qkv[:, 0:2, D:QKV]
        rden = sb("rden", [P, 2, SPAN, HG])
        attn = xnT[:, :, :].rearrange("p c t -> p (c t)")
        attnT = w_qkv[:, 0:2, 0:D]
        gated = w_qkv[:, 2:4, 0:D]

        bank = ctx.enter_context(nc.psum_tensor("bank", [P, 8, 512], F32))
        banks_flat = bank[:, :, :].rearrange("p b n -> p (b n)")

        x_in = [sem(f"x_in{t}") for t in range(NT)]
        wqkv_in, wout_in, wlin_in, rope_in, out_done = map(sem, ("wqkv_in", "wout_in", "wlin_in", "rope_in", "out_done"))
        zeroed, ident_ready, causal_ready, ones_ready = map(sem, ("zeroed", "ident_ready", "causal_ready", "ones_ready"))
        stats_done, mean_done, eps_done, std_done, rstd_done, xn_done = map(
            sem, ("stats_done", "mean_done", "eps_done", "std_done", "rstd_done", "xn_done"))
        quant_step, signs_done, quant_done = map(sem, ("quant_step", "signs_done", "quant_done"))
        turned, turn_copied, qkv_done = map(sem, ("turned", "turn_copied", "qkv_done"))
        rope_done, roped_done, high_done, rest_done, mid_done, low_done = map(
            sem, ("rope_done", "roped_done", "high_done", "rest_done", "mid_done", "low_done"))
        stacked, stack_out_a, stack_out_v = map(sem, ("stacked", "stack_out_a", "stack_out_v"))
        z_done, tanh_done, gate_done = map(sem, ("z_done", "tanh_done", "gate_done"))
        max_scored, max_taken, split_step, row_turned, row_placed = map(
            sem, ("max_scored", "max_taken", "split_step", "row_turned", "row_placed"))
        v_loaded, scored, exp_done, masked, valued, acc_drained, acc_turned, rden_done, divided = map(
            sem, ("v_loaded", "scored", "exp_done", "masked", "valued", "acc_drained", "acc_turned", "rden_done", "divided"))
        pool_passed, dve_passed = sem("pool_passed"), sem("dve_passed")
        merged, merge_copied, projected, gated_done, summed = map(
            sem, ("merged", "merge_copied", "projected", "gated_done", "summed"))

        def q_rows(p1, g, j, s, n=1):
            return qst[0:p1, bass.ds((g * HG + j) * T + s * P, n * P)]

        def k_rows(p1, g, kt, n=1):
            return kst[0:p1, bass.ds(g * T + kt * P, n * P)]

        def tile_no(g, s):
            return g * NT + s

        def pair_no(g, b, kt):
            return g * len(PAIRS) + PAIRS.index((b, kt))

        def chunk_no(g, s, half, j):
            return g * CHUNKS + chunks_before(s) + half * HG + j

        def heads(ap):
            return ap.rearrange("p (h d) -> p h d", d=HD)

        def z_bank(t):
            return Z_BANKS[t % 2 if t >= DC else 0]

        def stack_src(n, b):
            flat = bank[0:KS, STACK_BANKS[n % 2], :].bitcast(BF16)
            return flat.rearrange("p (h n) -> p h n", h=8)

        def stack_dst(t, b):
            to, first = (qst, 8 * b) if b < NH // 8 else (kst, 0)
            return to[0:KS, :].rearrange("p (h t) -> p h t", t=T)[:, first:first + 8, t * P:(t + 1) * P]

        block = ctx.enter_context(nc.Block())

        @block.sync
        def _(sp):
            x_rows = x.rearrange("a (t p) d -> p (a t) d", p=P)
            for t in range(2):
                sp.dma_start(x_sb[:, t, :], x_rows[:, t, :]).then_inc(x_in[t], 16)
            sp.dma_start(w_qkv[:, :, 0:D], wq.rearrange("(c p) n -> p c n", p=P)).then_inc(wqkv_in, 16)
            for t in range(2, 4):
                sp.dma_start(x_sb[:, t, :], x_rows[:, t, :]).then_inc(x_in[t], 16)
            sp.dma_start(w_lin[:, :, :], weight.rearrange("(c p) n -> p c n", p=P)).then_inc(wlin_in, 16)
            for t in range(4, NT):
                sp.dma_start(x_sb[:, t, :], x_rows[:, t, :]).then_inc(x_in[t], 16)
            sp.wait_ge(z_done, NT)
            sp.dma_start(w_out[:, :, :], wo.rearrange("(c p) n -> p c n", p=P)).then_inc(wout_in, 16)
            out_rows = out.rearrange("a (t p) d -> p (a t) d", p=P)
            for t in range(NT):
                sp.wait_ge(summed, t + 1)
                sp.dma_start(out_rows[:, t, :], x_sb[:, t, :]).then_inc(out_done, 16)
            sp.wait_ge(out_done, 16 * NT)

        @block.gpsimd
        def _(pool):
            pool.memset(v_grp[:, :, HD:2 * HD], 1.0).then_inc(ones_ready, 1)
            for m in (ident, ident_b, causal):
                pool.memset(m[:, :], 0.0).then_inc(zeroed, 1)
            pool.wait_ge(zeroed, 3)
            for m in (ident, ident_b):
                pool.affine_select(out=m[:, :], in_=m[:, :], compare_op=ALU.not_equal, fill=1.0, base=0,
                                   pattern=[[-1, P]], channel_multiplier=1).then_inc(ident_ready, 1)
            last_tile = causal[:, (SPAN - 1) * P:SPAN * P]
            pool.affine_select(out=last_tile, in_=last_tile, compare_op=ALU.is_ge, fill=LOWEST, base=0,
                               pattern=[[-1, P]], channel_multiplier=1).then_inc(causal_ready, 1)
            pool.wait_ge(causal_ready, 1)
            pool.memset(kst[KS:KM, :], 1.0).then_inc(ones_ready, 1)
            pool.wait_ge(ones_ready, 2)

            def quantise(c):
                pool.wait_ge(signs_done, c + 1)
                pool.tensor_tensor(w_lin[:, c, :], w_pos[:, :], w_neg[:, :], ALU.subtract).then_inc(quant_done, 1)

            def split(g, s, early=False):
                n = tile_no(g, s)
                pool.wait_ge(max_taken, chunk_no(g, s, *max_chunks(s)[-1]) + 1)
                wait(pool, row_turned, n - 1)
                pass_waits(pool, pool_passed)
                t0, t1 = top[:, s % 2, s // SPAN, :], top_rest[:, s % 2, :]
                part = [top_parts[:, s % 2, :, i] for i in range(3)]
                pool.tensor_scalar(part[0], t0, -1.0, None, ALU.mult).then_inc(split_step, 1)
                pool.wait_ge(split_step, n * 5 + 1)
                pool.tensor_tensor(t1, t0, part[0], ALU.add).then_inc(split_step, 1)
                pool.wait_ge(split_step, n * 5 + 2)
                pass_waits(pool, pool_passed)
                pool.tensor_scalar(part[1], t1, -1.0, None, ALU.mult).then_inc(split_step, 1)
                pool.wait_ge(split_step, n * 5 + 3)
                pool.tensor_tensor(t1, t1, part[1], ALU.add).then_inc(split_step, 1)
                pool.wait_ge(split_step, n * 5 + 4)
                pass_waits(pool, pool_passed)
                pool.tensor_scalar(part[2], t1, -1.0, None, ALU.mult).then_inc(split_step, 1)

            first = {"split": split}
            for t in range(NT):
                early(first, WITH_PROJECTION.get(t))
                pool.wait_ge(rope_done, t + 1)
                if t >= 1:
                    pool.wait_ge(high_done, t)
                pool.tensor_tensor(roped[:, :], rope_a[:, :], rope_b[:, :], ALU.add).then_inc(roped_done, 1)
                if t < DC:
                    quantise(t)
                early(first, WITH_LINEAR.get(t - DC))
                pool.wait_ge(mid_done, t + 1)
                stk = parts[:, t % 2]
                pool.tensor_tensor(stk[:, 0:NH, 5, :], heads(rest[:, 0:D]), stk[:, 0:NH, 3, :], ALU.subtract)
                pool.tensor_tensor(stk[:, NH:QKH, 2, :], heads(rest[:, D:QK]), stk[:, NH:QKH, 1, :],
                                   ALU.subtract).then_inc(low_done, 1)

            early(first, WITH_LINEAR[NT - DC])
            early(first, WITH_LINEAR[NT - DC + 1])

            def load(g, half):
                wait(pool, valued, pair_no(g - 1, NB - 1, (half + 1) * SPAN - 1) + 1)
                n = SPAN * HD
                pool.tensor_copy(v_grp[:, half * SPAN:(half + 1) * SPAN, 0:HD],
                                 heads(v_all[:, bass.ds(g * (2 * n) + half * n, n)])).then_inc(v_loaded, 1)

            def mask(g, b, kt):
                n = pair_no(g, b, kt)
                pool.wait_ge(exp_done, (n + 1) * HG)
                pass_waits(pool, pool_passed)
                at = 512 - queries(b, kt)
                p = probs[:, PAIRS.index((b, kt)) % PROBS, :, at:at + P]
                pool.affine_select(out=p, in_=p, compare_op=ALU.is_ge, fill=0.0, base=0,
                                   pattern=[[0, HG], [1, P]], channel_multiplier=-1).then_inc(masked, 1)

            steps = {"split": split, "load": load, "mask": mask}
            pool.wait_ge(rope_done, NT)
            prologue(steps)
            attention(pool, steps)

        @block.scalar
        def _(act):
            for w, lo, hi in ((wk, D, QK), (wv, QK, QKV)):
                act.dma_start(w_qkv[:, :, lo:hi], w.rearrange("(c p) n -> p c n", p=P)).then_inc(wqkv_in, 16)
            for sbuf, dram in ((cos_sb, rope_cos), (sin_sb, rope_sin)):
                act.dma_start(sbuf[:, :, :], dram).then_inc(rope_in, 16)

            def deviation(t):
                act.wait_ge(eps_done, t + 1)
                act.activation(std[:, t:t + 1], var_eps[:, t:t + 1], ACT.Sqrt).then_inc(std_done, 1)

            turn_count = 0

            def turn_out(dst):
                nonlocal turn_count
                act.wait_ge(turned, turn_count + 1)
                src = bank[:, TURN_BANKS[turn_count % 2], :].rearrange("p (c n) -> p c n", c=DC)
                act.activation(dst, src, ACT.Copy).then_inc(turn_copied, 1)
                turn_count += 1

            def x_out(t):
                turn_out(xnT[:, :, t * P:(t + 1) * P])

            def high(t):
                act.wait_ge(roped_done, t + 1)
                if t >= 2:
                    act.wait_ge(stacked, QKH // 8 * (t - 1))
                stk = parts[:, t % 2]
                q, k = heads(roped[:, 0:D]).unsqueeze(2), heads(roped[:, D:QK]).unsqueeze(2)
                act.activation(stk[:, 0:NH, 0:3, :], q.broadcast_to([P, NH, 3, HD]), ACT.Copy)
                act.activation(stk[:, NH:QKH, 0:4:3, :], k.broadcast_to([P, NG, 2, HD]), ACT.Copy)
                act.activation(stk[:, NH:QKH, 5:6, :], k, ACT.Copy).then_inc(high_done, 1)

            def stack_batch_out(t, b):
                n = t * (QKH // 8) + b
                if n % 2 == 0:
                    act.wait_ge(stacked, n + 1)
                    act.activation(stack_dst(t, b), stack_src(n, b), ACT.Copy).then_inc(stack_out_a, 1)

            def stack_out(t, portion):
                for b in range(QKH // 8):
                    if b > 1 or not out_ahead(t):
                        stack_batch_out(t, b)
                    early(first, portion, (b,))

            def z_tanh(t):
                act.wait_ge(z_done, t + 1)
                if t >= 2:
                    act.wait_ge(gate_done, t - 1)
                act.activation(tanh_z[:, t % 2, :], bank[:, z_bank(t), :], ACT.Tanh, scale=0.5).then_inc(tanh_done, 1)

            def place_rows(g, s, early=False):
                act.wait_ge(row_turned, tile_no(g, s) + 1)
                to = qst[KS:KM, bass.ds(g * (HG * T), HG * T)].rearrange("p (h t) -> p h t", h=HG)
                rows = bank[KS:KM, EARLY_BANK if early else SMALL_BANK, 0:HG * P // 2].bitcast(BF16).rearrange("p (h t) -> p h t", h=HG)
                act.activation(to[:, :, s * P:(s + 1) * P], rows, ACT.Copy).then_inc(row_placed, 1)

            first = {"row": place_rows}
            act.wait_ge(zeroed, 1)
            act.activation(std[:, NT - 1:NT], v_grp[:, 0, HD:HD + 1], ACT.Sqrt)
            deviation(0)
            deviation(1)
            deviation(2)
            x_out(0)
            x_out(1)
            for t in range(NT):
                if t >= 2:
                    stack_out(t - 2, WITH_PROJECTION.get(t))
                if t < NT // 2 - 1:
                    deviation(2 * t + 3)
                    x_out(2 * t + 2)
                    x_out(2 * t + 3)
                if 1 <= t <= DC:
                    turn_out(w_linT[:, :, (t - 1) * P:t * P])
                early(first, WITH_LINEAR.get(t - DC))
                if t < NT // 2 - 2:
                    deviation(2 * t + 4)
                if t >= 1 and out_ahead(t - 1):
                    stack_batch_out(t - 1, 0)
                    stack_batch_out(t - 1, 1)
                high(t)
                if t >= DC:
                    z_tanh(t - DC)
            for t in (NT - 2, NT - 1):
                stack_out(t, WITH_LINEAR[t - 2])
                z_tanh(t - 2)

            def exponential(g, b, kt, j):
                n, i = pair_no(g, b, kt), PAIRS.index((b, kt))
                act.wait_ge(scored, n * HG + j + 1)
                if j == 0:
                    wait(act, valued, n + 1 - PROBS)
                w = queries(b, kt)
                act.activation(probs[:, i % PROBS, j, 512 - w:512], bank[:, SCORE_BANKS[(i * HG + j) % 3], 0:w],
                               ACT.Exp, scale=SM_SCALE).then_inc(exp_done, 1)

            def drain(g, b):
                act.wait_ge(valued, pair_no(g, b, SPAN * (b + 1) - 1) + 1)
                wait(act, acc_turned, g * NB + b)
                act.activation(drained, bank[:, ACC_BANK, :].rearrange("p (a n) -> p a n", a=2), ACT.Copy).then_inc(acc_drained, 1)

            steps = {"score": exponential, "row": place_rows, "drain": drain}
            prologue(steps, z_tanh)
            attention(act, steps)
        @block.vector
        def _(dve):
            def normalise(t):
                dve.wait_ge(x_in[t], 16)
                dve.bn_stats(stats[:, t, :], x_sb[:, t, :]).then_inc(stats_done, 1)
                dve.wait_ge(stats_done, t + 1)
                dve.bn_aggr(mean_var[:, t, :], stats[:, t, :]).then_inc(mean_done, 1)
                dve.wait_ge(mean_done, t + 1)
                dve.tensor_scalar(var_eps[:, t:t + 1], mean_var[:, t, 1:2], LN_EPS, None, ALU.add).then_inc(eps_done, 1)
                dve.wait_ge(std_done, t + 1)
                dve.reciprocal(rstd[:, t:t + 1], std[:, t:t + 1]).then_inc(rstd_done, 1)
                dve.wait_ge(rstd_done, t + 1)
                if t >= 2:
                    dve.wait_ge(turned, x_turns_before(t - 2) + 1)
                dve.tensor_scalar(xn[:, t % 2, :], x_sb[:, t, :], mean_var[:, t, 0:1], rstd[:, t:t + 1],
                                  ALU.subtract, ALU.mult).then_inc(xn_done, 1)

            def quantise(c):
                if c >= 1:
                    dve.wait_ge(quant_done, c)
                for i in range(NQ):
                    n, cols = c * NQ + i, slice(i * QUANT, (i + 1) * QUANT)
                    dve.tensor_scalar(w_pos[:, cols], w_lin[:, c, cols], q_above[:, n:n + 1], q_scale[:, n:n + 1],
                                      ALU.is_gt, ALU.mult)
                    last = dve.tensor_scalar(w_neg[:, cols], w_lin[:, c, cols], q_below[:, n:n + 1],
                                             q_scale[:, n:n + 1], ALU.is_lt, ALU.mult)
                last.then_inc(signs_done, 1)

            def maximum(g, s, half, j, early=False):
                n, c = tile_no(g, s), chunk_no(g, s, half, j)
                dve.wait_ge(max_scored, c + 1)
                if (half, j) == (0, 0):
                    wait(dve, split_step, (n - 1) * 5)
                i = (chunks_before(s) + half * HG + j) % 3
                b = EARLY_BANK if early else MAX_BANKS[i]
                tiles = s + 1 - half * SPAN
                to = top[:, s % 2, half, j:j + 1]
                if tiles > SPAN:
                    dve.tensor_reduce(to, bank[:, b, :], AX.X, ALU.max).then_inc(max_taken, 1)
                    return
                start = LOWEST
                if half:
                    dve.wait_ge(max_taken, chunk_no(g, s, 0, j) + 1)
                    start = top[:, s % 2, 0, j:j + 1]
                pass_waits(dve, dve_passed)
                w = tiles * P
                to_see = seen_early[:, 0:w] if early else seen[:, i, 0:w]
                dve.tensor_tensor_reduce(to_see, bank[:, b, 0:w], causal[:, SPAN * P - w:], 1.0, start,
                                         ALU.add, ALU.max, to).then_inc(max_taken, 1)

            for t in range(4):
                normalise(t)
            dve.wait_ge(wlin_in, 16)
            dve.tensor_reduce(q_sum[:, :], w_lin[:, :, :].rearrange("p c (n k) -> p (c n) k", k=QUANT), AX.X, ALU.add,
                              apply_absolute_value=True).then_inc(quant_step, 1)
            dve.wait_ge(quant_step, 1)
            dve.tensor_scalar(q_scale[:, :], q_sum[:, :], 1.0 / QUANT, SCALE_EPS, ALU.mult, ALU.max).then_inc(quant_step, 1)
            dve.wait_ge(quant_step, 2)
            dve.tensor_scalar(q_above[:, :], q_scale[:, :], THRESHOLD, None, ALU.mult).then_inc(quant_step, 1)
            dve.tensor_scalar(q_below[:, :], q_scale[:, :], -THRESHOLD, None, ALU.mult).then_inc(quant_step, 1)
            dve.wait_ge(quant_step, 4)

            def rotate(t):
                dve.wait_ge(qkv_done, t + 1)
                b = PROJ_BANKS[t % 2] * 512
                qk = heads(banks_flat[:, b:b + QK])
                a, r = heads(rope_a[:, :]), heads(rope_b[:, :])

                def over_heads(table, lo, hi):
                    return table[:, t, lo:hi].unsqueeze(1).broadcast_to([P, QKH, hi - lo])

                dve.tensor_tensor(a, qk, over_heads(cos_sb, 0, HD), ALU.mult)
                dve.tensor_tensor(r[:, :, 0:HALF], qk[:, :, HALF:HD], over_heads(sin_sb, 0, HALF), ALU.mult)
                dve.tensor_tensor(r[:, :, HALF:HD], qk[:, :, 0:HALF], over_heads(sin_sb, HALF, HD), ALU.mult)
                v = v_all[:, :].rearrange("p (g t d) -> p g t d", g=NG, t=NT)[:, :, t, 0:HD]
                dve.tensor_copy(v, heads(banks_flat[:, b + QK:b + QKV])).then_inc(rope_done, 1)

            def mid(t):
                dve.wait_ge(high_done, t + 1)
                if t >= 1:
                    dve.wait_ge(low_done, t)
                stk = parts[:, t % 2]
                dve.tensor_tensor(heads(rest[:, :]), heads(roped[:, :]), stk[:, :, 0, :], ALU.subtract).then_inc(rest_done, 1)
                dve.wait_ge(rest_done, t + 1)
                q, k = heads(rest[:, 0:D]).unsqueeze(2), heads(rest[:, D:QK]).unsqueeze(2)
                dve.tensor_copy(stk[:, 0:NH, 3:5, :], q.broadcast_to([P, NH, 2, HD]))
                dve.tensor_copy(stk[:, NH:QKH, 1:5:3, :], k.broadcast_to([P, NG, 2, HD])).then_inc(mid_done, 1)

            def stack_batch_out(t, b):
                n = t * (QKH // 8) + b
                if n % 2 == 1:
                    dve.wait_ge(stacked, n + 1)
                    dve.tensor_copy(stack_dst(t, b), stack_src(n, b)).then_inc(stack_out_v, 1)

            def stack_out(t, portion):
                for b in range(QKH // 8):
                    if b > 1 or not out_ahead(t):
                        stack_batch_out(t, b)
                    early(first, portion, (b,))

            def gating(t):
                dve.wait_ge(tanh_done, t + 1)
                dve.scalar_tensor_tensor(gate[:, t, :], tanh_z[:, t % 2, :], 1.0, bank[:, z_bank(t), :],
                                         ALU.add, ALU.mult).then_inc(gate_done, 1)

            first = {"max": maximum}
            dve.wait_ge(causal_ready, 1)
            dve.wait_ge(rope_in, 32)
            for t in range(NT):
                if t >= 2:
                    stack_out(t - 2, WITH_PROJECTION.get(t))
                if 1 <= t < NT // 2 - 1:
                    normalise(2 * t + 3)
                rotate(t)
                if t < NT // 2 - 2:
                    normalise(2 * t + 4)
                if t < DC:
                    quantise(t)
                early(first, WITH_LINEAR.get(t - DC))
                if t >= 1 and out_ahead(t - 1):
                    stack_batch_out(t - 1, 0)
                    stack_batch_out(t - 1, 1)
                mid(t)
                if t >= DC:
                    gating(t - DC)
            for t in (NT - 2, NT - 1):
                stack_out(t, WITH_LINEAR[t - 2])
                gating(t - 2)

            def divide(g, b):
                n = g * NB + b
                dve.wait_ge(acc_turned, n + 1)
                res = bank[:, SMALL_BANK, :].rearrange("p (t h d) -> p t h d", t=SPAN, h=HG)
                r = rden[:, b, :, :]
                dve.reciprocal(r, res[:, :, :, HD]).then_inc(rden_done, 1)
                dve.wait_ge(rden_done, n + 1)
                to = attn[:, bass.ds(g * (HG * HD) + b * (SPAN * D), (SPAN - 1) * D + HG * HD)]
                to = attn_block(to)
                dve.tensor_tensor(to, res[:, :, :, 0:HD], r.unsqueeze(3).broadcast_to([P, SPAN, HG, HD]),
                                  ALU.mult).then_inc(divided, 1)

            def merge(_, t):
                dve.wait_ge(merged, t + 1)
                if t >= 2:
                    dve.wait_ge(projected, t - 1)
                dve.tensor_copy(attnT[:, t % 2, :], bank[:, MERGE_BANK, :]).then_inc(merge_copied, 1)

            def finish(_, t):
                dve.wait_ge(projected, t + 1)
                dve.scalar_tensor_tensor(gated[:, t % 2, :], bank[:, OUT_BANKS[t % 2], :], 0.5, gate[:, t, :],
                                         ALU.mult, ALU.mult).then_inc(gated_done, 1)
                dve.wait_ge(gated_done, t + 1)
                dve.tensor_tensor(x_sb[:, t, :], gated[:, t % 2, :], x_sb[:, t, :], ALU.add).then_inc(summed, 1)

            steps = {"max": maximum, "turn": divide, "merge": merge, "finish": finish}
            prologue(steps, gating)
            attention(dve, steps)

        @block.tensor
        def _(pe):
            turn_count = 0

            def turn(src):
                nonlocal turn_count
                wait(pe, turn_copied, turn_count - 1)
                for c in range(DC):
                    last = pe.transpose(bank[:, TURN_BANKS[turn_count % 2], c * P:(c + 1) * P],
                                        src[:, c * P:(c + 1) * P], ident[:, :])
                last.then_inc(turned, 1)
                turn_count += 1

            def x_turn(t):
                pe.wait_ge(xn_done, t + 1)
                turn(xn[:, t % 2, :])

            def project(t, stacks=None):
                pe.wait_ge(turn_copied, x_turns_before(t) + 1)
                if t >= 2:
                    pe.wait_ge(rope_done, t - 1)
                b, portion = PROJ_BANKS[t % 2], WITH_PROJECTION.get(t)
                for lo, hi, dst in ((0, D, b), (D, QKV, b + 1)):
                    for c in range(DC):
                        if stacks is not None and (lo == 0 or c == 0):
                            stack(stacks, c + DC * (lo > 0))
                        last = pe.matmul(bank[:, dst, 0:hi - lo], xnT[:, c, t * P:(t + 1) * P], w_qkv[:, c, lo:hi],
                                         start=(c == 0), stop=(c == DC - 1))
                        if (lo, c) == (D, DC - 1):
                            last.then_inc(qkv_done, 1)
                        if lo == 0 or c == 1:
                            early(first, portion, (c if lo == 0 else DC,))

            def linear(t, stacks=None):
                if t == 0:
                    pe.wait_ge(turn_copied, turn_count)
                wait(pe, gate_done, t if t < DC + 1 else t - 1)
                portion = WITH_LINEAR.get(t)
                for c in range(DC):
                    if stacks is not None:
                        stack(stacks, c)
                    last = pe.matmul(bank[:, z_bank(t), :], xnT[:, c, t * P:(t + 1) * P], w_linT[:, c, :],
                                     start=(c == 0), stop=(c == DC - 1))
                    if c == DC - 1:
                        last.then_inc(z_done, 1)
                    early(first, portion, (c,))
                if stacks is not None:
                    stack(stacks, DC)
                early(first, portion, (DC,))

            def stack(t, b):
                if b == 0:
                    pe.wait_ge(low_done, t + 1)
                    pe.wait_ge(mid_done, t + 1)
                    pe.wait_ge(high_done, t + 1)
                n = t * (QKH // 8) + b
                wait(pe, stack_out_v if n % 2 else stack_out_a, n // 2)
                dst = bank[0:KS, STACK_BANKS[n % 2], :].bitcast(BF16)
                for i in range(8):
                    last = pe.transpose(dst[:, i * P:(i + 1) * P],
                                        parts[:, t % 2, 8 * b + i].rearrange("p n d -> p (n d)"), ident_b[:, :])
                last.then_inc(stacked, 1)

            chunks_out = rows_out = 0

            def stacks_needed(s):
                n = (s + 1) * (QKH // 8)
                pe.wait_ge(stack_out_a, (n + 1) // 2)
                pe.wait_ge(stack_out_v, n // 2)

            def early_bank_free(chunks):
                pe.wait_ge(turn_copied, NT + DC - 1)
                wait(pe, max_taken, chunks)
                wait(pe, row_placed, rows_out)

            def score_for_max(g, s, half, j, early=False):
                nonlocal chunks_out
                c = chunks_before(s) + half * HG + j
                b = EARLY_BANK if early else MAX_BANKS[c % 3]
                if early:
                    stacks_needed(s)
                    early_bank_free(c)
                    chunks_out = c + 1
                else:
                    wait(pe, max_taken, chunk_no(g, s, half, j) - 2)
                n = min(s + 1 - half * SPAN, SPAN)
                pe.matmul(bank[:, b, 0:n * P], q_rows(KS, g, j, s), k_rows(KS, g, half * SPAN, n),
                          start=True, stop=True).then_inc(max_scored, 1)

            def small_bank_free(g, kind, s):
                at = time_of(kind, s)
                rows = g * NT + issued_before("row", at, NT)
                wait(pe, row_placed, min(rows, NG * NT) if isinstance(g, int) else rows)
                wait(pe, divided, g * NB + issued_before("turn", at, NB))

            def turn_rows(g, s, early=False):
                nonlocal rows_out
                n = tile_no(g, s)
                pe.wait_ge(split_step, (n + 1) * 5)
                if early:
                    early_bank_free(chunks_out)
                    rows_out = s + 1
                else:
                    small_bank_free(g, "row", s)
                dst = bank[KS:KM, EARLY_BANK if early else SMALL_BANK, 0:HG * P // 2].bitcast(BF16)
                for j in range(HG):
                    last = pe.transpose(dst[:, j * P:(j + 1) * P], top_parts[:, s % 2, j, :], ident_b[:, :])
                last.then_inc(row_turned, 1)

            first = {"max": score_for_max, "row": turn_rows}
            pe.wait_ge(ident_ready, 2)
            x_turn(0)
            x_turn(1)
            pe.wait_ge(wqkv_in, 48)
            for t in range(NT):
                project(t, t - 2 if t >= 2 else None)
                if t < NT // 2 - 1:
                    x_turn(2 * t + 2)
                    x_turn(2 * t + 3)
                if 1 <= t <= DC:
                    pe.wait_ge(quant_done, t)
                    turn(w_lin[:, t - 1, :])
                if t >= DC:
                    linear(t - DC)
            linear(NT - DC, NT - 2)
            linear(NT - DC + 1, NT - 1)

            def score(g, b, kt, j):
                n, i = pair_no(g, b, kt), PAIRS.index((b, kt)) * HG + j
                if kt == 0 and j == 0:
                    pe.wait_ge(row_placed, tile_no(g, SPAN * (b + 1)))
                wait(pe, exp_done, n * HG + j - 2)
                w = queries(b, kt)
                pe.matmul(bank[:, SCORE_BANKS[i % 3], 0:w], k_rows(KM, g, kt),
                          q_rows(KM, g, j, SPAN * (b + 1) - w // P, w // P),
                          start=True, stop=True).then_inc(scored, 1)

            def value(g, b, kt):
                n, i = pair_no(g, b, kt), PAIRS.index((b, kt))
                if kt == 0:
                    wait(pe, acc_drained, g * NB + b)
                if b == kt // SPAN and kt % SPAN == 0:
                    pe.wait_ge(v_loaded, NB * g + b + 1)
                pe.wait_ge(exp_done, (n + 1) * HG)
                if kt >= SPAN * b:
                    pe.wait_ge(masked, g * NT + kt + 1)
                w = queries(b, kt)
                for j in range(HG):
                    last = pe.matmul(bank[j * 2 * HD:(j + 1) * 2 * HD, ACC_BANK, 512 - w:512], v_grp[:, kt, :],
                                     probs[:, i % PROBS, j, 512 - w:512], start=(kt == 0),
                                     stop=(kt == SPAN * (b + 1) - 1))
                last.then_inc(valued, 1)

            def turn_back(g, b):
                pe.wait_ge(acc_drained, g * NB + b + 1)
                small_bank_free(g, "turn", b)
                for i in range(SPAN):
                    last = pe.transpose(bank[:, SMALL_BANK, i * P:(i + 1) * P], drained[:, i // 2, i % 2 * P:(i % 2 + 1) * P],
                                        ident[:, :])
                last.then_inc(acc_turned, 1)

            def merge(_, t):
                pe.wait_ge(divided, NG * NB - (t < SPAN))
                pe.wait_ge(max_taken, NG * CHUNKS)
                wait(pe, merge_copied, t)
                for c in range(DC):
                    last = pe.transpose(bank[:, MERGE_BANK, c * P:(c + 1) * P],
                                        attn[:, t * D + c * P:t * D + (c + 1) * P], ident[:, :])
                last.then_inc(merged, 1)

            def finish(_, t):
                if t == 0:
                    pe.wait_ge(wout_in, 16)
                pe.wait_ge(merge_copied, t + 1)
                wait(pe, gated_done, t - 1)
                for c in range(DC):
                    last = pe.matmul(bank[:, OUT_BANKS[t % 2], :], attnT[:, t % 2, c * P:(c + 1) * P], w_out[:, c, :],
                                     start=(c == 0), stop=(c == DC - 1))
                last.then_inc(projected, 1)

            steps = {"max": score_for_max, "row": turn_rows, "score": score, "value": value, "turn": turn_back,
                     "merge": merge, "finish": finish}
            pe.wait_ge(stack_out_a, NT * (QKH // 8) // 2)
            pe.wait_ge(stack_out_v, NT * (QKH // 8) // 2)
            pe.wait_ge(ones_ready, 2)
            prologue(steps, linear)
            pe.wait_ge(gate_done, NT)
            attention(pe, steps)


def out_ahead(t):
    return t < DC - 1


def x_turns_before(t):
    return t + max(0, t // 2 - 2)


def rope_tables():
    inv = (1.0 / ROPE_BASE ** (np.arange(0, HD, 2, dtype=np.float32) / np.float32(HD))).astype(np.float32)
    freqs = np.arange(T, dtype=np.float32)[:, None] * inv[None, :]
    cos, sin = np.cos(freqs).astype(np.float32), np.sin(freqs).astype(np.float32)

    def by_tile(a):
        return np.ascontiguousarray(a.reshape(NT, P, HD).transpose(1, 0, 2))
    return by_tile(np.concatenate([cos, cos], 1)), by_tile(np.concatenate([-sin, sin], 1))


_INS = ["L0_attn_x", "L0_attn_Wq", "L0_attn_Wk", "L0_attn_Wv", "L0_attn_Wo", "L0_ffn_weight"]


def kernel(**inputs):
    import concourse.bacc as bacc
    from concourse.bass_utils import run_bass_kernel_spmd

    nc = bacc.Bacc("TRN2", target_bir_lowering=False, num_devices=1)
    arrays = {name: np.ascontiguousarray(inputs[name]) for name in _INS}
    arrays["rope_cos"], arrays["rope_sin"] = rope_tables()
    args = [nc.dram_tensor(name, a.shape, mybir.dt.from_np(a.dtype), kind="ExternalInput").ap()
            for name, a in arrays.items()]
    out = nc.dram_tensor("out", (1, T, D), F32, kind="ExternalOutput").ap()
    build(nc, *args, out)
    got = run_bass_kernel_spmd(nc, [arrays], core_ids=[0])
    return got.results[0]["out"]
```

```python
from contextlib import ExitStack

import numpy as np

import concourse.bass as bass
from concourse import mybir

F32 = mybir.dt.float32
BF16 = mybir.dt.bfloat16
ALU = mybir.AluOpType
ACT = mybir.ActivationFunctionType
AX = mybir.AxisListType

P = 128
D = 512
DC = D // P
T = 1024
NT = T // P
NH = 32
NG = 8
HG = NH // NG
HD = D // NH
HALF = HD // 2
QK = D + NG * HD
QKV = QK + NG * HD
QKH = NH + NG
NPROD = 6
KS = NPROD * HD
KM = KS + 3
QUANT = 128
NQ = D // QUANT
THRESHOLD = 0.5
SCALE_EPS = 1e-8
LN_EPS = 1e-5
SM_SCALE = 1.0 / float(np.sqrt(HD))
LOWEST = -3.0e38
ROPE_BASE = 500000.0
SPAN = 512 // P
NB = NT // SPAN

Q_SLOT = (0, 0, 0, 1, 1, 2)
K_SLOT = (0, 1, 2, 0, 1, 0)

TURN_BANKS = (0, 5)
EARLY_BANK = 0
Z_BANKS = (5, 1)
PROJ_BANKS = (1, 3)
STACK_BANKS = (6, 7)
SCORE_BANKS = (0, 1, 2)
MAX_BANKS = (3, 4, 7)
ACC_BANK = 5
SMALL_BANK = 6
MERGE_BANK = 3
OUT_BANKS = (4, 7)

PROBS = 3


PAIRS = [(b, kt) for b in range(NB) for kt in range(SPAN * (b + 1))]


def queries(b, kt):
    return min(SPAN, SPAN * (b + 1) - kt) * P


FIXED = 0.12
SCORE_TIME = [queries(*pair) / 512 + FIXED for pair in PAIRS for _ in range(HG)]
GROUP_TIME = sum(SCORE_TIME)
BLOCK_START = [sum(SCORE_TIME[:PAIRS.index((b, 0)) * HG]) for b in range(NB)]
MAX_SHARE = (1.0, 1.05, 1.0, 1.0, 1.0, 1.0, 1.0, 1.0)
ROW_LAG = (3.53, 3.53, 4.53, 4.53, 3.53, 3.53, 4.53, 3.53)
VALUE_LAG = (4, 6, 4, 4, 4, 5, 5, 4, 4, 5, 4, 4)
DRAIN_LAG = 0.05
TURN_LAG = (5.5, 4.5)
SLACK = 0.75
LEAD = GROUP_TIME - BLOCK_START[-1] + ROW_LAG[-1] + SLACK


def score_start(i):
    again, i = divmod(i, len(SCORE_TIME))
    return again * GROUP_TIME + sum(SCORE_TIME[:i])


def max_chunks(s):
    return [(half, j) for half in range(s // SPAN + 1) for j in range(HG)]


def chunks_before(s):
    return sum(len(max_chunks(r)) for r in range(s))


CHUNKS = chunks_before(NT)


def attention_steps():
    steps = []
    cost = {(s, half, j): (min(s + 1 - half * SPAN, SPAN) * P / 0.96 + 70) * MAX_SHARE[s]
            for s in range(NT) for half, j in max_chunks(s)}
    whole, at = sum(cost.values()), 0.0
    for (s, half, j), c in cost.items():
        steps.append((at / whole * GROUP_TIME - LEAD, "max", (s, half, j)))
        at += c
        if (half, j) == max_chunks(s)[-1]:
            steps.append((at / whole * GROUP_TIME - LEAD, "split", (s,)))
            steps.append((at / whole * GROUP_TIME - LEAD + ROW_LAG[s], "row", (s,)))
    for n, (b, kt) in enumerate(PAIRS):
        for j in range(HG):
            steps.append((score_start(n * HG + j), "score", (b, kt, j)))
        if kt >= SPAN * b:
            steps.append((score_start((n + 1) * HG) - 0.01, "mask", (b, kt)))
        at = score_start((n + 1) * HG + VALUE_LAG[n]) - 0.01
        steps.append((at, "value", (b, kt)))
        if kt == SPAN * (b + 1) - 1:
            steps.append((at + DRAIN_LAG, "drain", (b,)))
            steps.append((at + DRAIN_LAG + TURN_LAG[b], "turn", (b,)))
        if b == NB - 1 and kt % SPAN == SPAN - 1:
            steps.append((at + 0.02 - GROUP_TIME, "load", (kt // SPAN,)))
    return sorted(steps, key=lambda x: x[0])


STEPS = attention_steps()


def steps_within(start, stop, spans, more=()):
    found = [(time + GROUP_TIME * dg, dg, kind, args) for dg in spans for time, kind, args in STEPS
             if start <= time + GROUP_TIME * dg < stop]
    found += [(time, 0, kind, args) for time, kind, args in more if start <= time < stop]
    return [x[1:] for x in sorted(found, key=lambda x: x[0])]


def time_of(kind, s):
    return next(time for time, k, args in STEPS if k == kind and args == (s,))


FIRST_TURN = time_of("drain", 0) + 4
PARTS = [(t, 0, DC) for t in range(SPAN)] + [(t, 0, DC - 1) for t in range(SPAN, NT)]
PARTS += [(t, DC - 1, DC) for t in range(SPAN, NT)]
PART_STEP = (2.9, 0.6)
PART_LAG = 3.0
PART_START = [FIRST_TURN + 0.3 + i * PART_STEP[0] for i in range(NT)]
PART_START += [time_of("turn", 1) + 0.3 + i * PART_STEP[1] for i in range(SPAN)]
TAIL = [(FIRST_TURN, "turn", (0,))]
for _k, _at in enumerate(PART_START):
    _next = PART_START[min(_k + 1, len(PARTS) - 1)]
    TAIL += [(_at, "merge", (_k,)), (min(_next, _at + PART_LAG) + 0.05, "finish", (_k,))]


def last_part(t):
    return max(k for k, part in enumerate(PARTS) if part[0] == t)


EARLY_HALVES = ((0, 0), (1, 0), (2, 0), (3, 0), (4, 0), (4, 1), (5, 0), (5, 1), (6, 0))
WITH_PROJECTION = {5: 1, 6: 3, 7: 5}
WITH_LINEAR = {0: 0, 1: 2, 2: 4, 3: 6, 4: 7, 5: 8}
PROJECTION_SLOTS = ((), (0,), (1,), (2,), (3, 4))
LINEAR_SLOTS = ((0,), (1,), (2,), (3,), (4,))


def complete(half):
    return half[0] // SPAN == half[1]


def early_portion(n):
    s, half = EARLY_HALVES[n]
    turned = n >= 2 and complete(EARLY_HALVES[n - 2])
    slots = [[("row", (EARLY_HALVES[n - 2][0],))] if turned else []]
    slots += [[("max", (s, half, j))] for j in range(HG)]
    if complete((s, half)):
        slots[-1].append(("split", (s,)))
    return slots


EARLY = [early_portion(n) for n in range(len(EARLY_HALVES))]
EARLY_STEPS = [step for portion in EARLY for slot in portion for step in slot]
PROLOGUE = [x for x in steps_within(-GROUP_TIME, 0, (0,)) if x[1:] not in EARLY_STEPS]
FIRST_BODY = steps_within(0, GROUP_TIME, (0, 1))
BODY = steps_within(0, GROUP_TIME, (-1, 0, 1))
LAST_BODY = steps_within(0, GROUP_TIME, (-1, 0), TAIL)
del LAST_BODY[max(i for i, step in enumerate(LAST_BODY) if step == (0, "turn", (0,)))]
EPILOGUE = steps_within(GROUP_TIME, 2 * GROUP_TIME, (0,), TAIL)


def issued_before(kind, at, per_group):
    return sum(time + GROUP_TIME * dg < at for dg in (-1, 0, 1) for time, k, _ in STEPS if k == kind) - per_group


def attention(eng, steps):
    def walk(plan, g):
        for dg, kind, args in plan:
            if kind in steps:
                steps[kind](g + dg, *args)

    walk(FIRST_BODY, 0)
    with eng.Fori(1, NG - 1) as g:
        walk(BODY, g)
    walk(LAST_BODY, NG - 1)
    walk(EPILOGUE, NG - 1)


def early(steps, portion, slots=range(HG + 1)):
    if portion is not None:
        for slot in slots:
            for kind, args in EARLY[portion][slot]:
                if kind in steps:
                    steps[kind](0, *args, early=True)


def prologue(steps, linear=None):
    for i, (_, kind, args) in enumerate(PROLOGUE):
        if linear and i in (0, len(PROLOGUE) // 2):
            linear(NT - 2 + (i > 0))
        if kind in steps:
            steps[kind](0, *args)


def wait(eng, sem, value):
    if not isinstance(value, int) or value > 0:
        eng.wait_ge(sem, value)


def pass_waits(eng, sem):
    eng.sem_inc(sem, 1)


def attn_block(ap):
    return bass.AP(ap.tensor, ap.offset, [ap.ap[0], [D, SPAN], [HD, HG], [1, HD]])


def build(nc, x, wq, wk, wv, wo, weight, rope_cos, rope_sin, out):
    with ExitStack() as ctx:
        def sb(name, shape, dt=F32):
            return ctx.enter_context(nc.sbuf_tensor(name, shape, dt))

        def sem(name):
            return ctx.enter_context(nc.semaphore(name))

        x_sb = sb("x_sb", [P, NT, D])
        xn = sb("xn", [P, 2, D])
        xnT = sb("xnT", [P, DC, T])
        w_qkv = sb("w_qkv", [P, DC, QKV])
        probs = sb("probs", [P, PROBS, HG, 512])
        room = probs[:, :, :, :].rearrange("p b h n -> p (b h n)")
        sizes = (DC * D, D, D, QK, QK, QK, QK)
        starts = [sum(sizes[:i]) for i in range(len(sizes))]
        w_lin, w_pos, w_neg, rope_a, rope_b, roped, rest = [room[:, a:a + n] for a, n in zip(starts, sizes)]
        w_lin = w_lin.rearrange("p (c d) -> p c d", c=DC)
        w_linT = sb("w_linT", [P, DC, D])
        w_out = w_linT
        cos_sb = sb("cos_sb", [P, NT, HD])
        sin_sb = sb("sin_sb", [P, NT, HD])
        gate = sb("gate", [P, NT, D])
        qst = sb("qst", [KM, NH * T], BF16)
        kst = sb("kst", [KM, NG * T], BF16)
        v_all = sb("v_all", [P, NG * NT * HD])
        v_grp = sb("v_grp", [P, NT, 2 * HD])
        ident = sb("ident", [P, P])
        ident_b = sb("ident_b", [P, P], BF16)
        causal = sb("causal", [P, SPAN * P])
        stats = sb("stats", [P, NT, 6])
        mean_var = sb("mean_var", [P, NT, 2])
        var_eps = sb("var_eps", [P, NT])
        std = sb("std", [P, NT])
        rstd = sb("rstd", [P, NT])
        q_sum = sb("q_sum", [P, DC * NQ])
        q_scale = sb("q_scale", [P, DC * NQ])
        q_above = sb("q_above", [P, DC * NQ])
        q_below = sb("q_below", [P, DC * NQ])
        parts = sb("parts", [P, 2, QKH, NPROD, HD], BF16)
        seen_early = sb("seen_early", [P, 512])
        tanh_z = sb("tanh_z", [P, 2, D])
        top = sb("top", [P, 2, 2, HG])
        top_rest = sb("top_rest", [P, 2, HG])
        top_parts = sb("top_parts", [P, 2, HG, 3], BF16)
        seen = w_qkv[:, 0:3, 0:D]
        drained = w_qkv[:, 0:2, D:QKV]
        rden = sb("rden", [P, 2, SPAN, HG])
        attn = xnT[:, :, :].rearrange("p c t -> p (c t)")
        attnT = w_qkv[:, 0:2, 0:D]
        gated = w_qkv[:, 2:4, 0:D]

        bank = ctx.enter_context(nc.psum_tensor("bank", [P, 8, 512], F32))
        banks_flat = bank[:, :, :].rearrange("p b n -> p (b n)")

        x_in = [sem(f"x_in{t}") for t in range(NT)]
        wqkv_in, wout_in, wlin_in, rope_in, out_done = map(sem, ("wqkv_in", "wout_in", "wlin_in", "rope_in", "out_done"))
        zeroed, ident_ready, causal_ready, ones_ready = map(sem, ("zeroed", "ident_ready", "causal_ready", "ones_ready"))
        stats_done, mean_done, eps_done, std_done, rstd_done, xn_done = map(
            sem, ("stats_done", "mean_done", "eps_done", "std_done", "rstd_done", "xn_done"))
        quant_step, signs_done, quant_done = map(sem, ("quant_step", "signs_done", "quant_done"))
        turned, turn_copied, qkv_done = map(sem, ("turned", "turn_copied", "qkv_done"))
        rope_done, roped_done, high_done, rest_done, mid_done, low_done = map(
            sem, ("rope_done", "roped_done", "high_done", "rest_done", "mid_done", "low_done"))
        stacked, stack_out_a, stack_out_v = map(sem, ("stacked", "stack_out_a", "stack_out_v"))
        z_done, tanh_done, gate_done = map(sem, ("z_done", "tanh_done", "gate_done"))
        max_scored, max_taken, split_step, row_turned, row_placed = map(
            sem, ("max_scored", "max_taken", "split_step", "row_turned", "row_placed"))
        v_loaded, scored, exp_done, masked, valued, acc_drained, acc_turned, rden_done, divided = map(
            sem, ("v_loaded", "scored", "exp_done", "masked", "valued", "acc_drained", "acc_turned", "rden_done", "divided"))
        pool_passed, dve_passed = sem("pool_passed"), sem("dve_passed")
        merged, merge_copied, projected, gated_done, summed = map(
            sem, ("merged", "merge_copied", "projected", "gated_done", "summed"))

        def q_rows(p1, g, j, s, n=1):
            return qst[0:p1, bass.ds((g * HG + j) * T + s * P, n * P)]

        def k_rows(p1, g, kt, n=1):
            return kst[0:p1, bass.ds(g * T + kt * P, n * P)]

        def tile_no(g, s):
            return g * NT + s

        def pair_no(g, b, kt):
            return g * len(PAIRS) + PAIRS.index((b, kt))

        def chunk_no(g, s, half, j):
            return g * CHUNKS + chunks_before(s) + half * HG + j

        def heads(ap):
            return ap.rearrange("p (h d) -> p h d", d=HD)

        def z_bank(t):
            return Z_BANKS[(t + 1) % 2 if t >= DC else 0]

        def stack_src(n, b):
            flat = bank[0:KS, STACK_BANKS[n % 2], :].bitcast(BF16)
            return flat.rearrange("p (h n) -> p h n", h=8)

        def stack_dst(t, b):
            to, first = (qst, 8 * b) if b < NH // 8 else (kst, 0)
            return to[0:KS, :].rearrange("p (h t) -> p h t", t=T)[:, first:first + 8, t * P:(t + 1) * P]

        block = ctx.enter_context(nc.Block())

        @block.sync
        def _(sp):
            x_rows = x.rearrange("a (t p) d -> p (a t) d", p=P)
            for t in range(2):
                sp.dma_start(x_sb[:, t, :], x_rows[:, t, :]).then_inc(x_in[t], 16)
            sp.dma_start(w_qkv[:, :, 0:D], wq.rearrange("(c p) n -> p c n", p=P)).then_inc(wqkv_in, 16)
            for t in range(2, 4):
                sp.dma_start(x_sb[:, t, :], x_rows[:, t, :]).then_inc(x_in[t], 16)
            sp.dma_start(w_lin[:, :, :], weight.rearrange("(c p) n -> p c n", p=P)).then_inc(wlin_in, 16)
            for t in range(4, NT):
                sp.dma_start(x_sb[:, t, :], x_rows[:, t, :]).then_inc(x_in[t], 16)
            sp.wait_ge(z_done, NT)
            sp.dma_start(w_out[:, :, :], wo.rearrange("(c p) n -> p c n", p=P)).then_inc(wout_in, 16)
            out_rows = out.rearrange("a (t p) d -> p (a t) d", p=P)
            for t in range(NT):
                sp.wait_ge(summed, last_part(t) + 1)
                sp.dma_start(out_rows[:, t, :], x_sb[:, t, :]).then_inc(out_done, 16)
            sp.wait_ge(out_done, 16 * NT)

        @block.gpsimd
        def _(pool):
            pool.memset(v_grp[:, :, HD:2 * HD], 1.0).then_inc(ones_ready, 1)
            for m in (ident, ident_b, causal):
                pool.memset(m[:, :], 0.0).then_inc(zeroed, 1)
            pool.wait_ge(zeroed, 3)
            for m in (ident, ident_b):
                pool.affine_select(out=m[:, :], in_=m[:, :], compare_op=ALU.not_equal, fill=1.0, base=0,
                                   pattern=[[-1, P]], channel_multiplier=1).then_inc(ident_ready, 1)
            last_tile = causal[:, (SPAN - 1) * P:SPAN * P]
            pool.affine_select(out=last_tile, in_=last_tile, compare_op=ALU.is_ge, fill=LOWEST, base=0,
                               pattern=[[-1, P]], channel_multiplier=1).then_inc(causal_ready, 1)
            pool.wait_ge(causal_ready, 1)
            pool.memset(kst[KS:KM, :], 1.0).then_inc(ones_ready, 1)
            pool.wait_ge(ones_ready, 2)

            def quantise(c):
                pool.wait_ge(signs_done, c + 1)
                pool.tensor_tensor(w_lin[:, c, :], w_pos[:, :], w_neg[:, :], ALU.subtract).then_inc(quant_done, 1)

            def split(g, s, early=False):
                n = tile_no(g, s)
                pool.wait_ge(max_taken, chunk_no(g, s, *max_chunks(s)[-1]) + 1)
                wait(pool, row_turned, n - 1)
                pass_waits(pool, pool_passed)
                t0, t1 = top[:, s % 2, s // SPAN, :], top_rest[:, s % 2, :]
                part = [top_parts[:, s % 2, :, i] for i in range(3)]
                pool.tensor_scalar(part[0], t0, -1.0, None, ALU.mult).then_inc(split_step, 1)
                pool.wait_ge(split_step, n * 5 + 1)
                pool.tensor_tensor(t1, t0, part[0], ALU.add).then_inc(split_step, 1)
                pool.wait_ge(split_step, n * 5 + 2)
                pass_waits(pool, pool_passed)
                pool.tensor_scalar(part[1], t1, -1.0, None, ALU.mult).then_inc(split_step, 1)
                pool.wait_ge(split_step, n * 5 + 3)
                pool.tensor_tensor(t1, t1, part[1], ALU.add).then_inc(split_step, 1)
                pool.wait_ge(split_step, n * 5 + 4)
                pass_waits(pool, pool_passed)
                pool.tensor_scalar(part[2], t1, -1.0, None, ALU.mult).then_inc(split_step, 1)

            first = {"split": split}
            for t in range(NT):
                early(first, WITH_PROJECTION.get(t))
                pool.wait_ge(rope_done, t + 1)
                if t >= 1:
                    pool.wait_ge(high_done, t)
                pool.tensor_tensor(roped[:, :], rope_a[:, :], rope_b[:, :], ALU.add).then_inc(roped_done, 1)
                if t < DC:
                    quantise(t)
                early(first, WITH_LINEAR.get(t - DC))
                pool.wait_ge(mid_done, t + 1)
                stk = parts[:, t % 2]
                pool.tensor_tensor(stk[:, 0:NH, 5, :], heads(rest[:, 0:D]), stk[:, 0:NH, 3, :], ALU.subtract)
                pool.tensor_tensor(stk[:, NH:QKH, 2, :], heads(rest[:, D:QK]), stk[:, NH:QKH, 1, :],
                                   ALU.subtract).then_inc(low_done, 1)

            for t in (DC, DC + 1):
                early(first, WITH_LINEAR[t])

            def load(g, half):
                wait(pool, valued, pair_no(g - 1, NB - 1, (half + 1) * SPAN - 1) + 1)
                n = SPAN * HD
                pool.tensor_copy(v_grp[:, half * SPAN:(half + 1) * SPAN, 0:HD],
                                 heads(v_all[:, bass.ds(g * (2 * n) + half * n, n)])).then_inc(v_loaded, 1)

            def mask(g, b, kt):
                n = pair_no(g, b, kt)
                pool.wait_ge(exp_done, (n + 1) * HG)
                pass_waits(pool, pool_passed)
                at = 512 - queries(b, kt)
                p = probs[:, PAIRS.index((b, kt)) % PROBS, :, at:at + P]
                pool.affine_select(out=p, in_=p, compare_op=ALU.is_ge, fill=0.0, base=0,
                                   pattern=[[0, HG], [1, P]], channel_multiplier=-1).then_inc(masked, 1)

            steps = {"split": split, "load": load, "mask": mask}
            pool.wait_ge(rope_done, NT)
            prologue(steps)
            attention(pool, steps)

        @block.scalar
        def _(act):
            for w, lo, hi in ((wk, D, QK), (wv, QK, QKV)):
                act.dma_start(w_qkv[:, :, lo:hi], w.rearrange("(c p) n -> p c n", p=P)).then_inc(wqkv_in, 16)
            for sbuf, dram in ((cos_sb, rope_cos), (sin_sb, rope_sin)):
                act.dma_start(sbuf[:, :, :], dram).then_inc(rope_in, 16)

            def deviation(t):
                act.wait_ge(eps_done, t + 1)
                act.activation(std[:, t:t + 1], var_eps[:, t:t + 1], ACT.Sqrt).then_inc(std_done, 1)

            turn_count = 0

            def turn_out(dst):
                nonlocal turn_count
                act.wait_ge(turned, turn_count + 1)
                src = bank[:, TURN_BANKS[turn_count % 2], :].rearrange("p (c n) -> p c n", c=DC)
                act.activation(dst, src, ACT.Copy).then_inc(turn_copied, 1)
                turn_count += 1

            def x_out(t):
                turn_out(xnT[:, :, t * P:(t + 1) * P])

            def high(t):
                act.wait_ge(roped_done, t + 1)
                if t >= 2:
                    act.wait_ge(stacked, QKH // 8 * (t - 1))
                stk = parts[:, t % 2]
                q, k = heads(roped[:, 0:D]).unsqueeze(2), heads(roped[:, D:QK]).unsqueeze(2)
                act.activation(stk[:, 0:NH, 0:3, :], q.broadcast_to([P, NH, 3, HD]), ACT.Copy)
                act.activation(stk[:, NH:QKH, 0:4:3, :], k.broadcast_to([P, NG, 2, HD]), ACT.Copy)
                act.activation(stk[:, NH:QKH, 5:6, :], k, ACT.Copy).then_inc(high_done, 1)

            def stack_batch_out(t, b):
                n = t * (QKH // 8) + b
                if n % 2 == 0:
                    act.wait_ge(stacked, n + 1)
                    act.activation(stack_dst(t, b), stack_src(n, b), ACT.Copy).then_inc(stack_out_a, 1)

            def stack_out(t, portion, slots):
                for b in range(QKH // 8):
                    if b > 1 or t >= DC - 1:
                        stack_batch_out(t, b)
                    early(first, portion, slots[b])

            def z_tanh(t):
                act.wait_ge(z_done, t + 1)
                if t >= 2:
                    act.wait_ge(gate_done, t - 1)
                act.activation(tanh_z[:, t % 2, :], bank[:, z_bank(t), :], ACT.Tanh, scale=0.5).then_inc(tanh_done, 1)

            def place_rows(g, s, early=False):
                act.wait_ge(row_turned, tile_no(g, s) + 1)
                to = qst[KS:KM, bass.ds(g * (HG * T), HG * T)].rearrange("p (h t) -> p h t", h=HG)
                rows = bank[KS:KM, EARLY_BANK if early else SMALL_BANK, 0:HG * P // 2].bitcast(BF16).rearrange("p (h t) -> p h t", h=HG)
                act.activation(to[:, :, s * P:(s + 1) * P], rows, ACT.Copy).then_inc(row_placed, 1)

            first = {"row": place_rows}
            act.wait_ge(ones_ready, 1)
            act.activation(std[:, NT - 1:NT], v_grp[:, 0, HD:HD + 1], ACT.Sqrt)
            deviation(0)
            deviation(1)
            x_out(0)
            x_out(1)
            deviation(2)
            deviation(3)
            for t in range(NT):
                if t >= 2:
                    stack_out(t - 2, WITH_PROJECTION.get(t), PROJECTION_SLOTS)
                if t == 0:
                    x_out(2)
                if t <= NT - 4:
                    x_out(t + 3)
                if 1 <= t <= DC:
                    turn_out(w_linT[:, :, (t - 1) * P:t * P])
                early(first, WITH_LINEAR.get(t - DC))
                if t + 4 < NT:
                    deviation(t + 4)
                if 1 <= t < DC:
                    stack_batch_out(t - 1, 0)
                    stack_batch_out(t - 1, 1)
                high(t)
                if t >= DC:
                    z_tanh(t - DC)
            for t in (NT - 2, NT - 1):
                stack_out(t, WITH_LINEAR[t - 2], LINEAR_SLOTS)
                z_tanh(t - 2)

            def exponential(g, b, kt, j):
                n, i = pair_no(g, b, kt), PAIRS.index((b, kt))
                act.wait_ge(scored, n * HG + j + 1)
                if j == 0:
                    wait(act, valued, n + 1 - PROBS)
                w = queries(b, kt)
                act.activation(probs[:, i % PROBS, j, 512 - w:512], bank[:, SCORE_BANKS[(i * HG + j) % 3], 0:w],
                               ACT.Exp, scale=SM_SCALE).then_inc(exp_done, 1)

            def drain(g, b):
                act.wait_ge(valued, pair_no(g, b, SPAN * (b + 1) - 1) + 1)
                wait(act, acc_turned, g * NB + b)
                act.activation(drained, bank[:, ACC_BANK, :].rearrange("p (a n) -> p a n", a=2), ACT.Copy).then_inc(acc_drained, 1)

            steps = {"score": exponential, "row": place_rows, "drain": drain}
            prologue(steps, z_tanh)
            attention(act, steps)

        @block.vector
        def _(dve):
            def normalise(t):
                dve.wait_ge(x_in[t], 16)
                dve.bn_stats(stats[:, t, :], x_sb[:, t, :]).then_inc(stats_done, 1)
                dve.wait_ge(stats_done, t + 1)
                dve.bn_aggr(mean_var[:, t, :], stats[:, t, :]).then_inc(mean_done, 1)
                dve.wait_ge(mean_done, t + 1)
                dve.tensor_scalar(var_eps[:, t:t + 1], mean_var[:, t, 1:2], LN_EPS, None, ALU.add).then_inc(eps_done, 1)
                dve.wait_ge(std_done, t + 1)
                dve.reciprocal(rstd[:, t:t + 1], std[:, t:t + 1]).then_inc(rstd_done, 1)
                dve.wait_ge(rstd_done, t + 1)
                if t >= 2:
                    dve.wait_ge(turned, x_turns_before(t - 2) + 1)
                dve.tensor_scalar(xn[:, t % 2, :], x_sb[:, t, :], mean_var[:, t, 0:1], rstd[:, t:t + 1],
                                  ALU.subtract, ALU.mult).then_inc(xn_done, 1)

            def quantise(c):
                if c >= 1:
                    dve.wait_ge(quant_done, c)
                for i in range(NQ):
                    n, cols = c * NQ + i, slice(i * QUANT, (i + 1) * QUANT)
                    dve.tensor_scalar(w_pos[:, cols], w_lin[:, c, cols], q_above[:, n:n + 1], q_scale[:, n:n + 1],
                                      ALU.is_gt, ALU.mult)
                    last = dve.tensor_scalar(w_neg[:, cols], w_lin[:, c, cols], q_below[:, n:n + 1],
                                             q_scale[:, n:n + 1], ALU.is_lt, ALU.mult)
                last.then_inc(signs_done, 1)

            def maximum(g, s, half, j, early=False):
                n, c = tile_no(g, s), chunk_no(g, s, half, j)
                dve.wait_ge(max_scored, c + 1)
                if (half, j) == (0, 0):
                    wait(dve, split_step, (n - 1) * 5)
                i = (chunks_before(s) + half * HG + j) % 3
                b = EARLY_BANK if early else MAX_BANKS[i]
                tiles = s + 1 - half * SPAN
                to = top[:, s % 2, half, j:j + 1]
                if tiles > SPAN:
                    dve.tensor_reduce(to, bank[:, b, :], AX.X, ALU.max).then_inc(max_taken, 1)
                    return
                start = LOWEST
                if half:
                    dve.wait_ge(max_taken, chunk_no(g, s, 0, j) + 1)
                    start = top[:, s % 2, 0, j:j + 1]
                pass_waits(dve, dve_passed)
                w = tiles * P
                to_see = seen_early[:, 0:w] if early else seen[:, i, 0:w]
                dve.tensor_tensor_reduce(to_see, bank[:, b, 0:w], causal[:, SPAN * P - w:], 1.0, start,
                                         ALU.add, ALU.max, to).then_inc(max_taken, 1)

            for t in range(4):
                normalise(t)
            dve.wait_ge(wlin_in, 16)
            dve.tensor_reduce(q_sum[:, :], w_lin[:, :, :].rearrange("p c (n k) -> p (c n) k", k=QUANT), AX.X, ALU.add,
                              apply_absolute_value=True).then_inc(quant_step, 1)
            dve.wait_ge(quant_step, 1)
            dve.tensor_scalar(q_scale[:, :], q_sum[:, :], 1.0 / QUANT, SCALE_EPS, ALU.mult, ALU.max).then_inc(quant_step, 1)
            dve.wait_ge(quant_step, 2)
            dve.tensor_scalar(q_above[:, :], q_scale[:, :], THRESHOLD, None, ALU.mult).then_inc(quant_step, 1)
            dve.tensor_scalar(q_below[:, :], q_scale[:, :], -THRESHOLD, None, ALU.mult).then_inc(quant_step, 1)
            dve.wait_ge(quant_step, 4)

            def rotate(t):
                dve.wait_ge(qkv_done, t + 1)
                b = PROJ_BANKS[t % 2] * 512
                qk = heads(banks_flat[:, b:b + QK])
                a, r = heads(rope_a[:, :]), heads(rope_b[:, :])

                def over_heads(table, lo, hi):
                    return table[:, t, lo:hi].unsqueeze(1).broadcast_to([P, QKH, hi - lo])

                dve.tensor_tensor(a, qk, over_heads(cos_sb, 0, HD), ALU.mult)
                dve.tensor_tensor(r[:, :, 0:HALF], qk[:, :, HALF:HD], over_heads(sin_sb, 0, HALF), ALU.mult)
                dve.tensor_tensor(r[:, :, HALF:HD], qk[:, :, 0:HALF], over_heads(sin_sb, HALF, HD), ALU.mult)
                v = v_all[:, :].rearrange("p (g t d) -> p g t d", g=NG, t=NT)[:, :, t, 0:HD]
                dve.tensor_copy(v, heads(banks_flat[:, b + QK:b + QKV])).then_inc(rope_done, 1)

            def mid(t):
                dve.wait_ge(high_done, t + 1)
                if t >= 1:
                    dve.wait_ge(low_done, t)
                stk = parts[:, t % 2]
                dve.tensor_tensor(heads(rest[:, :]), heads(roped[:, :]), stk[:, :, 0, :], ALU.subtract).then_inc(rest_done, 1)
                dve.wait_ge(rest_done, t + 1)
                q, k = heads(rest[:, 0:D]).unsqueeze(2), heads(rest[:, D:QK]).unsqueeze(2)
                dve.tensor_copy(stk[:, 0:NH, 3:5, :], q.broadcast_to([P, NH, 2, HD]))
                dve.tensor_copy(stk[:, NH:QKH, 1:5:3, :], k.broadcast_to([P, NG, 2, HD])).then_inc(mid_done, 1)

            def stack_batch_out(t, b):
                n = t * (QKH // 8) + b
                if n % 2 == 1:
                    dve.wait_ge(stacked, n + 1)
                    dve.tensor_copy(stack_dst(t, b), stack_src(n, b)).then_inc(stack_out_v, 1)

            def stack_out(t, portion, slots):
                for b in range(QKH // 8):
                    if b > 1 or b == 1 and t >= DC - 1 or t == NT - 1:
                        stack_batch_out(t, b)
                    early(first, portion, slots[b])

            def gating(t):
                dve.wait_ge(tanh_done, t + 1)
                dve.scalar_tensor_tensor(gate[:, t, :], tanh_z[:, t % 2, :], 1.0, bank[:, z_bank(t), :],
                                         ALU.add, ALU.mult).then_inc(gate_done, 1)

            first = {"max": maximum}
            dve.wait_ge(causal_ready, 1)
            dve.wait_ge(rope_in, 32)
            for t in range(NT):
                if t >= 2:
                    stack_out(t - 2, WITH_PROJECTION.get(t), PROJECTION_SLOTS)
                rotate(t)
                if t + 4 < NT:
                    normalise(t + 4)
                if 1 <= t < DC:
                    stack_batch_out(t - 1, 0)
                    stack_batch_out(t - 1, 1)
                if t < DC:
                    quantise(t)
                else:
                    early(first, WITH_LINEAR[t - DC], range(HG))
                    stack_batch_out(t - 1, 0)
                    early(first, WITH_LINEAR[t - DC], (HG,))
                mid(t)
                if t >= DC:
                    gating(t - DC)
            for t in (NT - 2, NT - 1):
                stack_out(t, WITH_LINEAR[t - 2], LINEAR_SLOTS)
                gating(t - 2)

            def divide(g, b):
                n = g * NB + b
                dve.wait_ge(acc_turned, n + 1)
                res = bank[:, SMALL_BANK, :].rearrange("p (t h d) -> p t h d", t=SPAN, h=HG)
                r = rden[:, b, :, :]
                dve.reciprocal(r, res[:, :, :, HD]).then_inc(rden_done, 1)
                dve.wait_ge(rden_done, n + 1)
                to = attn[:, bass.ds(g * (HG * HD) + b * (SPAN * D), (SPAN - 1) * D + HG * HD)]
                to = attn_block(to)
                dve.tensor_tensor(to, res[:, :, :, 0:HD], r.unsqueeze(3).broadcast_to([P, SPAN, HG, HD]),
                                  ALU.mult).then_inc(divided, 1)

            def merge(_, k):
                dve.wait_ge(merged, k + 1)
                if k >= 2:
                    dve.wait_ge(projected, k - 1)
                n = (PARTS[k][2] - PARTS[k][1]) * P
                dve.tensor_copy(attnT[:, k % 2, 0:n], bank[:, MERGE_BANK, 0:n]).then_inc(merge_copied, 1)

            def finish(_, k):
                t, first_chunk, _ = PARTS[k]
                dve.wait_ge(projected, k + 1)
                dve.scalar_tensor_tensor(gated[:, k % 2, :], bank[:, OUT_BANKS[k % 2], :], 0.5, gate[:, t, :],
                                         ALU.mult, ALU.mult).then_inc(gated_done, 1)
                dve.wait_ge(gated_done, k + 1)
                if first_chunk:
                    dve.wait_ge(summed, PARTS.index((t, 0, first_chunk)) + 1)
                dve.tensor_tensor(x_sb[:, t, :], gated[:, k % 2, :], x_sb[:, t, :], ALU.add).then_inc(summed, 1)

            steps = {"max": maximum, "turn": divide, "merge": merge, "finish": finish}
            prologue(steps, gating)
            attention(dve, steps)

        @block.tensor
        def _(pe):
            turn_count = 0

            def turn(src):
                nonlocal turn_count
                wait(pe, turn_copied, turn_count - 1)
                for c in range(DC):
                    last = pe.transpose(bank[:, TURN_BANKS[turn_count % 2], c * P:(c + 1) * P],
                                        src[:, c * P:(c + 1) * P], ident[:, :])
                last.then_inc(turned, 1)
                turn_count += 1

            def x_turn(t):
                pe.wait_ge(xn_done, t + 1)
                turn(xn[:, t % 2, :])

            def project(t, stacks=None):
                pe.wait_ge(turn_copied, x_turns_before(t) + 1)
                if t >= 2:
                    pe.wait_ge(rope_done, t - 1)
                b, portion = PROJ_BANKS[t % 2], WITH_PROJECTION.get(t)
                for lo, hi, dst in ((0, D, b), (D, QKV, b + 1)):
                    for c in range(DC):
                        if stacks is not None and (lo == 0 or c == 0):
                            stack(stacks, c + DC * (lo > 0))
                        last = pe.matmul(bank[:, dst, 0:hi - lo], xnT[:, c, t * P:(t + 1) * P], w_qkv[:, c, lo:hi],
                                         start=(c == 0), stop=(c == DC - 1))
                        if (lo, c) == (D, DC - 1):
                            last.then_inc(qkv_done, 1)
                        if (lo, c) == (0, 0):
                            early(first, WITH_LINEAR.get(t - 1 - DC), (DC,))
                        if lo == 0 and c > 0:
                            early(first, portion, (c - 1,))
                        if lo > 0 and c % 2 == 1:
                            early(first, portion, (DC - 1 + c // 2,))

            def linear(t, stacks=None):
                if t == 0:
                    pe.wait_ge(turn_copied, turn_count)
                if t == DC:
                    pe.wait_ge(rope_done, NT - 1)
                else:
                    wait(pe, gate_done, t if t < DC else t - 1)
                portion = WITH_LINEAR.get(t)
                for c in range(DC):
                    if stacks is not None:
                        stack(stacks, c)
                    last = pe.matmul(bank[:, z_bank(t), :], xnT[:, c, t * P:(t + 1) * P], w_linT[:, c, :],
                                     start=(c == 0), stop=(c == DC - 1))
                    if c == DC - 1:
                        last.then_inc(z_done, 1)
                    if stacks is not None and c == 0:
                        early(first, WITH_LINEAR[t - 1], (DC,))
                    early(first, portion, (c,))
                if stacks is not None:
                    stack(stacks, DC)

            def stack(t, b):
                if b == 0:
                    pe.wait_ge(low_done, t + 1)
                    pe.wait_ge(mid_done, t + 1)
                    pe.wait_ge(high_done, t + 1)
                n = t * (QKH // 8) + b
                wait(pe, stack_out_v if n % 2 else stack_out_a, n // 2)
                dst = bank[0:KS, STACK_BANKS[n % 2], :].bitcast(BF16)
                for i in range(8):
                    last = pe.transpose(dst[:, i * P:(i + 1) * P],
                                        parts[:, t % 2, 8 * b + i].rearrange("p n d -> p (n d)"), ident_b[:, :])
                last.then_inc(stacked, 1)

            chunks_out = rows_out = 0

            def stacks_needed(s):
                n = (s + 1) * (QKH // 8)
                pe.wait_ge(stack_out_a, (n + 1) // 2)
                pe.wait_ge(stack_out_v, n // 2)

            def early_bank_free(chunks):
                pe.wait_ge(turn_copied, TURNS)
                wait(pe, max_taken, chunks)
                wait(pe, row_placed, rows_out)

            def score_for_max(g, s, half, j, early=False):
                nonlocal chunks_out
                c = chunks_before(s) + half * HG + j
                b = EARLY_BANK if early else MAX_BANKS[c % 3]
                if early:
                    stacks_needed(s)
                    early_bank_free(c)
                    chunks_out = c + 1
                else:
                    wait(pe, max_taken, chunk_no(g, s, half, j) - 2)
                n = min(s + 1 - half * SPAN, SPAN)
                pe.matmul(bank[:, b, 0:n * P], q_rows(KS, g, j, s), k_rows(KS, g, half * SPAN, n),
                          start=True, stop=True).then_inc(max_scored, 1)

            def small_bank_free(g, kind, s):
                at = time_of(kind, s)
                rows = g * NT + issued_before("row", at, NT)
                wait(pe, row_placed, min(rows, NG * NT) if isinstance(g, int) else rows)
                wait(pe, divided, g * NB + issued_before("turn", at, NB))

            def turn_rows(g, s, early=False):
                nonlocal rows_out
                n = tile_no(g, s)
                pe.wait_ge(split_step, (n + 1) * 5)
                if early:
                    early_bank_free(chunks_out)
                    rows_out = s + 1
                else:
                    small_bank_free(g, "row", s)
                dst = bank[KS:KM, EARLY_BANK if early else SMALL_BANK, 0:HG * P // 2].bitcast(BF16)
                for j in range(HG):
                    last = pe.transpose(dst[:, j * P:(j + 1) * P], top_parts[:, s % 2, j, :], ident_b[:, :])
                last.then_inc(row_turned, 1)

            first = {"max": score_for_max, "row": turn_rows}
            pe.wait_ge(ident_ready, 2)
            x_turn(0)
            x_turn(1)
            pe.wait_ge(wqkv_in, 48)
            for t in range(NT):
                project(t, t - 2 if t >= 2 else None)
                if t == 0:
                    x_turn(2)
                if t <= NT - 4:
                    x_turn(t + 3)
                if 1 <= t <= DC:
                    pe.wait_ge(quant_done, t)
                    turn(w_lin[:, t - 1, :])
                if t >= DC:
                    linear(t - DC)
            linear(NT - DC, NT - 2)
            linear(NT - DC + 1, NT - 1)
            early(first, WITH_LINEAR[DC + 1], (DC,))

            def score(g, b, kt, j):
                n, i = pair_no(g, b, kt), PAIRS.index((b, kt)) * HG + j
                if kt == 0 and j == 0:
                    pe.wait_ge(row_placed, tile_no(g, SPAN * (b + 1)))
                wait(pe, exp_done, n * HG + j - 2)
                w = queries(b, kt)
                pe.matmul(bank[:, SCORE_BANKS[i % 3], 0:w], k_rows(KM, g, kt),
                          q_rows(KM, g, j, SPAN * (b + 1) - w // P, w // P),
                          start=True, stop=True).then_inc(scored, 1)

            def value(g, b, kt):
                n, i = pair_no(g, b, kt), PAIRS.index((b, kt))
                if kt == 0:
                    wait(pe, acc_drained, g * NB + b)
                if b == kt // SPAN and kt % SPAN == 0:
                    pe.wait_ge(v_loaded, NB * g + b + 1)
                pe.wait_ge(exp_done, (n + 1) * HG)
                if kt >= SPAN * b:
                    pe.wait_ge(masked, g * NT + kt + 1)
                w = queries(b, kt)
                for j in range(HG):
                    last = pe.matmul(bank[j * 2 * HD:(j + 1) * 2 * HD, ACC_BANK, 512 - w:512], v_grp[:, kt, :],
                                     probs[:, i % PROBS, j, 512 - w:512], start=(kt == 0),
                                     stop=(kt == SPAN * (b + 1) - 1))
                last.then_inc(valued, 1)

            def turn_back(g, b):
                pe.wait_ge(acc_drained, g * NB + b + 1)
                small_bank_free(g, "turn", b)
                for i in range(SPAN):
                    last = pe.transpose(bank[:, SMALL_BANK, i * P:(i + 1) * P], drained[:, i // 2, i % 2 * P:(i % 2 + 1) * P],
                                        ident[:, :])
                last.then_inc(acc_turned, 1)

            def merge(_, k):
                t, lo, hi = PARTS[k]
                pe.wait_ge(divided, NG // DC * hi * NB - (hi == DC and t < SPAN))
                pe.wait_ge(max_taken, NG * CHUNKS)
                wait(pe, merge_copied, k)
                for i, c in enumerate(range(lo, hi)):
                    last = pe.transpose(bank[:, MERGE_BANK, i * P:(i + 1) * P],
                                        attn[:, t * D + c * P:t * D + (c + 1) * P], ident[:, :])
                last.then_inc(merged, 1)

            def finish(_, k):
                _, lo, hi = PARTS[k]
                if k == 0:
                    pe.wait_ge(wout_in, 16)
                pe.wait_ge(merge_copied, k + 1)
                wait(pe, gated_done, k - 1)
                for i, c in enumerate(range(lo, hi)):
                    last = pe.matmul(bank[:, OUT_BANKS[k % 2], :], attnT[:, k % 2, i * P:(i + 1) * P], w_out[:, c, :],
                                     start=(c == lo), stop=(c == hi - 1))
                last.then_inc(projected, 1)

            steps = {"max": score_for_max, "row": turn_rows, "score": score, "value": value, "turn": turn_back,
                     "merge": merge, "finish": finish}
            pe.wait_ge(stack_out_a, NT * (QKH // 8) // 2)
            pe.wait_ge(stack_out_v, NT * (QKH // 8) // 2)
            pe.wait_ge(ones_ready, 2)
            prologue(steps, linear)
            pe.wait_ge(gate_done, NT)
            attention(pe, steps)


TURNS = NT + DC


def x_turns_before(t):
    return t + max(0, t - 4)


def rope_tables():
    inv = (1.0 / ROPE_BASE ** (np.arange(0, HD, 2, dtype=np.float32) / np.float32(HD))).astype(np.float32)
    freqs = np.arange(T, dtype=np.float32)[:, None] * inv[None, :]
    cos, sin = np.cos(freqs).astype(np.float32), np.sin(freqs).astype(np.float32)

    def by_tile(a):
        return np.ascontiguousarray(a.reshape(NT, P, HD).transpose(1, 0, 2))
    return by_tile(np.concatenate([cos, cos], 1)), by_tile(np.concatenate([-sin, sin], 1))


_INS = ["L0_attn_x", "L0_attn_Wq", "L0_attn_Wk", "L0_attn_Wv", "L0_attn_Wo", "L0_ffn_weight"]


def kernel(**inputs):
    import concourse.bacc as bacc
    from concourse.bass_utils import run_bass_kernel_spmd

    nc = bacc.Bacc("TRN2", target_bir_lowering=False, num_devices=1)
    arrays = {name: np.ascontiguousarray(inputs[name]) for name in _INS}
    arrays["rope_cos"], arrays["rope_sin"] = rope_tables()
    args = [nc.dram_tensor(name, a.shape, mybir.dt.from_np(a.dtype), kind="ExternalInput").ap()
            for name, a in arrays.items()]
    out = nc.dram_tensor("out", (1, T, D), F32, kind="ExternalOutput").ap()
    build(nc, *args, out)
    got = run_bass_kernel_spmd(nc, [arrays], core_ids=[0])
    return got.results[0]["out"]
```
